# Optimizing a Trainium2 kernel written in Bass

```python
import numpy as np
import jax
import jax.numpy as jnp

def _softmax(x, axis=-1):
    return jax.nn.softmax(x, axis=axis)

def _gelu(x):
    return jax.nn.gelu(x, approximate=True)

def _silu(x):
    return jax.nn.silu(x)

def _sigmoid(x):
    return jax.nn.sigmoid(x)

def _layernorm(x, axis=-1, eps=1e-05):
    m = jnp.mean(x, axis=axis, keepdims=True)
    v = jnp.var(x, axis=axis, keepdims=True)
    return (x - m) / jnp.sqrt(v + eps)

def _scatter_add(tgt, idx, src, axis=0):
    return tgt.at[idx].add(src)

def _segment_sum(src, seg, n):
    return jax.ops.segment_sum(src, seg, n)
kernel_name = 'mk_seq_preln_d2_jaxref_r4_7ef2dd'

def setup_inputs(seed: int=0):
    np.random.seed(seed)
    _w = jnp.asarray

    def _L0_attn_setup():
        import jax, jax.numpy as jnp
        import numpy as np
        key = jax.random.key(seed)
        k1, k2, k3 = jax.random.split(key, 3)
        N, S, D = (8, 512, 256)
        x = jax.random.normal(k1, (N, S, D), dtype=jnp.float32)
        std = np.sqrt(2.0 / D).astype(np.float32)
        w_lhs = jax.random.normal(k2, (1, 1, D), dtype=jnp.float32) * std
        w_rhs = jax.random.normal(k3, (1, 1, D), dtype=jnp.float32) * std
        return {'x': x, 'w_lhs': w_lhs, 'w_rhs': w_rhs}
    _L0_attn_in = _L0_attn_setup()

    def _L0_ffn_setup():
        import jax, jax.numpy as jnp
        import numpy as np
        FEATURES = 256
        D_IN = 256

        def fp8_gemm_optimized(x, input_scale, kernel, kernel_scale):
            s_in = input_scale[0]
            s_k = kernel_scale[0]
            x_q = (x.astype(jnp.float32) / s_in).astype(jnp.float8_e4m3fn)
            k_q = (kernel.astype(jnp.float32) / s_k).astype(jnp.float8_e4m3fn)
            y = jnp.dot(x_q.astype(jnp.float32), k_q.astype(jnp.float32), preferred_element_type=jnp.float32)
            return y * (s_in * s_k)
        key = jax.random.key(seed)
        kx, kk, kb = jax.random.split(key, 3)
        x = jax.random.normal(kx, (4, 2048, D_IN), dtype=jnp.float32)
        limit = np.sqrt(6.0 / (D_IN + FEATURES)).astype(np.float32)
        kernel = jax.random.uniform(kk, (D_IN, FEATURES), dtype=jnp.float32, minval=-limit, maxval=limit).astype(jnp.bfloat16)
        input_scale = jnp.ones((1,), dtype=jnp.float32)
        kernel_scale = jnp.ones((1,), dtype=jnp.float32)
        bias = jnp.zeros((FEATURES,), dtype=jnp.bfloat16)
        return {'x': x, 'kernel': kernel, 'input_scale': input_scale, 'kernel_scale': kernel_scale, 'bias': bias}
    _L0_ffn_in = _L0_ffn_setup()

    def _L1_attn_setup():
        import jax, jax.numpy as jnp
        import numpy as np
        from jax import lax
        D_MODEL = 256
        D_STATE = 16
        D_CONV = 4
        D_INNER = 2 * D_MODEL
        B_SZ = 2
        L_SEQ = 256
        EPS = 1e-05

        def _layernorm(x, w, b):
            mu = jnp.mean(x, axis=-1, keepdims=True)
            var = jnp.mean(jnp.square(x - mu), axis=-1, keepdims=True)
            return (x - mu) * lax.rsqrt(var + EPS) * w + b

        def _silu(x):
            return x * jax.nn.sigmoid(x)

        def _selective_scan(u, delta, A, B_ssm, C_ssm):
            dA = jnp.exp(delta[..., None] * A)
            dBu = (delta * u)[..., None] * B_ssm[:, :, None, :]
            dA_t = jnp.moveaxis(dA, 1, 0)
            dBu_t = jnp.moveaxis(dBu, 1, 0)
            C_t = jnp.moveaxis(C_ssm, 1, 0)

            def step(h, inp):
                dA_i, dBu_i, c_i = inp
                h = dA_i * h + dBu_i
                y = jnp.einsum('bds,bs->bd', h, c_i)
                return (h, y)
            h0 = jnp.zeros((u.shape[0], u.shape[2], A.shape[1]), u.dtype)
            _, ys = lax.scan(step, h0, (dA_t, dBu_t, C_t))
            return jnp.moveaxis(ys, 0, 1)
        key = jax.random.key(seed)
        ks = jax.random.split(key, 8)
        s = lambda k, shape, scale: jax.random.normal(k, shape, jnp.float32) * scale
        return {'x': jax.random.normal(ks[0], (B_SZ, L_SEQ, D_MODEL), jnp.float32), 'norm_w': jnp.ones((D_MODEL,), jnp.float32), 'norm_b': jnp.zeros((D_MODEL,), jnp.float32), 'in_proj_w': s(ks[1], (2 * D_INNER, D_MODEL), 0.02), 'in_proj_b': jnp.zeros((2 * D_INNER,), jnp.float32), 'conv_w': s(ks[2], (D_INNER, 1, D_CONV), 0.1), 'conv_b': jnp.zeros((D_INNER,), jnp.float32), 'x_proj_w': s(ks[3], (2 * D_STATE, D_INNER), 0.02), 'x_proj_b': jnp.zeros((2 * D_STATE,), jnp.float32), 'dt_proj_w': s(ks[4], (D_INNER, D_INNER), 0.02), 'dt_proj_b': jnp.zeros((D_INNER,), jnp.float32), 'A_log': s(ks[5], (D_INNER, D_STATE), 1.0), 'D_param': jnp.ones((D_INNER,), jnp.float32), 'out_proj_w': s(ks[6], (D_MODEL, D_INNER), 0.02), 'out_proj_b': jnp.zeros((D_MODEL,), jnp.float32)}
    _L1_attn_in = _L1_attn_setup()

    def _L1_ffn_setup():
        import jax, jax.numpy as jnp
        import numpy as np
        HIDDEN_SIZE = 256
        NUM_EXPERTS = 8
        MOE_INTERMEDIATE_SIZE = 352
        NUM_EXPERTS_PER_TOK = 2
        SHARED_EXPERT_INTERMEDIATE_SIZE = 704
        B, T = (2, 256)
        W_SCALE = 0.02
        key = jax.random.key(seed)
        ks = jax.random.split(key, 8)
        H, E, I, SI = (HIDDEN_SIZE, NUM_EXPERTS, MOE_INTERMEDIATE_SIZE, SHARED_EXPERT_INTERMEDIATE_SIZE)
        return {'x': jax.random.normal(ks[0], (B, T, H), jnp.float32), 'gate_w': jax.random.normal(ks[1], (E, H), jnp.float32) * W_SCALE, 'experts_gate_up': jax.random.normal(ks[2], (E, 2 * I, H), jnp.float32) * W_SCALE, 'experts_down': jax.random.normal(ks[3], (E, H, I), jnp.float32) * W_SCALE, 'shared_gate_w': jax.random.normal(ks[4], (SI, H), jnp.float32) * W_SCALE, 'shared_up_w': jax.random.normal(ks[5], (SI, H), jnp.float32) * W_SCALE, 'shared_down_w': jax.random.normal(ks[6], (H, SI), jnp.float32) * W_SCALE, 'shared_expert_gate_w': jax.random.normal(ks[7], (1, H), jnp.float32) * W_SCALE}
    _L1_ffn_in = _L1_ffn_setup()
    _d = {'L0_attn_x': _L0_attn_in['x'], 'L0_attn_w_lhs': _L0_attn_in['w_lhs'], 'L0_attn_w_rhs': _L0_attn_in['w_rhs'], 'L0_ffn_kernel': _L0_ffn_in['kernel'], 'L0_ffn_input_scale': _L0_ffn_in['input_scale'], 'L0_ffn_kernel_scale': _L0_ffn_in['kernel_scale'], 'L0_ffn_bias': _L0_ffn_in['bias'], 'L1_attn_norm_w': _L1_attn_in['norm_w'], 'L1_attn_norm_b': _L1_attn_in['norm_b'], 'L1_attn_in_proj_w': _L1_attn_in['in_proj_w'], 'L1_attn_in_proj_b': _L1_attn_in['in_proj_b'], 'L1_attn_conv_w': _L1_attn_in['conv_w'], 'L1_attn_conv_b': _L1_attn_in['conv_b'], 'L1_attn_x_proj_w': _L1_attn_in['x_proj_w'], 'L1_attn_x_proj_b': _L1_attn_in['x_proj_b'], 'L1_attn_dt_proj_w': _L1_attn_in['dt_proj_w'], 'L1_attn_dt_proj_b': _L1_attn_in['dt_proj_b'], 'L1_attn_A_log': _L1_attn_in['A_log'], 'L1_attn_D_param': _L1_attn_in['D_param'], 'L1_attn_out_proj_w': _L1_attn_in['out_proj_w'], 'L1_attn_out_proj_b': _L1_attn_in['out_proj_b'], 'L1_ffn_gate_w': _L1_ffn_in['gate_w'], 'L1_ffn_experts_gate_up': _L1_ffn_in['experts_gate_up'], 'L1_ffn_experts_down': _L1_ffn_in['experts_down'], 'L1_ffn_shared_gate_w': _L1_ffn_in['shared_gate_w'], 'L1_ffn_shared_up_w': _L1_ffn_in['shared_up_w'], 'L1_ffn_shared_down_w': _L1_ffn_in['shared_down_w'], 'L1_ffn_shared_expert_gate_w': _L1_ffn_in['shared_expert_gate_w']}
    _x0 = _d['L0_attn_x']
    _d['L0_attn_x'] = jax.random.normal(jax.random.fold_in(jax.random.key(seed), 1), (16, 512, 256), dtype=_x0.dtype)
    del _x0
    return _d

def reference(L0_attn_x, L0_attn_w_lhs, L0_attn_w_rhs, L0_ffn_kernel, L0_ffn_input_scale, L0_ffn_kernel_scale, L0_ffn_bias, L1_attn_norm_w, L1_attn_norm_b, L1_attn_in_proj_w, L1_attn_in_proj_b, L1_attn_conv_w, L1_attn_conv_b, L1_attn_x_proj_w, L1_attn_x_proj_b, L1_attn_dt_proj_w, L1_attn_dt_proj_b, L1_attn_A_log, L1_attn_D_param, L1_attn_out_proj_w, L1_attn_out_proj_b, L1_ffn_gate_w, L1_ffn_experts_gate_up, L1_ffn_experts_down, L1_ffn_shared_gate_w, L1_ffn_shared_up_w, L1_ffn_shared_down_w, L1_ffn_shared_expert_gate_w):

    def _L0_attn_ref(x, w_lhs, w_rhs):
        import jax, jax.numpy as jnp
        import numpy as np
        lhs = x * w_lhs
        rhs = x * w_rhs
        scores = jnp.einsum('nsd,ntd->nst', lhs, rhs)
        attn = jax.nn.softmax(scores, axis=2)
        return jnp.einsum('nst,ntd->nsd', attn, x)

    def _L0_ffn_ref(x, kernel, input_scale, kernel_scale, bias):
        import jax, jax.numpy as jnp
        import numpy as np
        FEATURES = 256
        D_IN = 256

        def fp8_gemm_optimized(x, input_scale, kernel, kernel_scale):
            s_in = input_scale[0]
            s_k = kernel_scale[0]
            x_q = (x.astype(jnp.float32) / s_in).astype(jnp.float8_e4m3fn)
            k_q = (kernel.astype(jnp.float32) / s_k).astype(jnp.float8_e4m3fn)
            y = jnp.dot(x_q.astype(jnp.float32), k_q.astype(jnp.float32), preferred_element_type=jnp.float32)
            return y * (s_in * s_k)
        dtype = jnp.bfloat16
        x = x.astype(dtype)
        orig_shape = x.shape
        x2 = x.reshape(-1, x.shape[-1])
        y = fp8_gemm_optimized(x2, input_scale, kernel, kernel_scale)
        y = y.astype(dtype) + bias
        return y.reshape(orig_shape[:-1] + (FEATURES,))

    def _L1_attn_ref(x, norm_w, norm_b, in_proj_w, in_proj_b, conv_w, conv_b, x_proj_w, x_proj_b, dt_proj_w, dt_proj_b, A_log, D_param, out_proj_w, out_proj_b):
        import jax, jax.numpy as jnp
        import numpy as np
        from jax import lax
        D_MODEL = 256
        D_STATE = 16
        D_CONV = 4
        D_INNER = 2 * D_MODEL
        B_SZ = 2
        L_SEQ = 256
        EPS = 1e-05

        def _layernorm(x, w, b):
            mu = jnp.mean(x, axis=-1, keepdims=True)
            var = jnp.mean(jnp.square(x - mu), axis=-1, keepdims=True)
            return (x - mu) * lax.rsqrt(var + EPS) * w + b

        def _silu(x):
            return x * jax.nn.sigmoid(x)

        def _selective_scan(u, delta, A, B_ssm, C_ssm):
            dA = jnp.exp(delta[..., None] * A)
            dBu = (delta * u)[..., None] * B_ssm[:, :, None, :]
            dA_t = jnp.moveaxis(dA, 1, 0)
            dBu_t = jnp.moveaxis(dBu, 1, 0)
            C_t = jnp.moveaxis(C_ssm, 1, 0)

            def step(h, inp):
                dA_i, dBu_i, c_i = inp
                h = dA_i * h + dBu_i
                y = jnp.einsum('bds,bs->bd', h, c_i)
                return (h, y)
            h0 = jnp.zeros((u.shape[0], u.shape[2], A.shape[1]), u.dtype)
            _, ys = lax.scan(step, h0, (dA_t, dBu_t, C_t))
            return jnp.moveaxis(ys, 0, 1)
        residual = x
        xn = _layernorm(x, norm_w, norm_b)
        xz = xn @ in_proj_w.T + in_proj_b
        xc, z = jnp.split(xz, 2, axis=-1)
        kern = jnp.transpose(conv_w, (2, 1, 0))
        xc = lax.conv_general_dilated(xc, kern, window_strides=(1,), padding=[(D_CONV - 1, 0)], dimension_numbers=('NLC', 'LIO', 'NLC'), feature_group_count=D_INNER) + conv_b
        u = _silu(xc)
        x_db = u @ x_proj_w.T + x_proj_b
        B_ssm, C_ssm = jnp.split(x_db, 2, axis=-1)
        delta = jax.nn.softplus(u @ dt_proj_w.T + dt_proj_b)
        A = -jnp.exp(A_log)
        y = _selective_scan(u, delta, A, B_ssm, C_ssm)
        y = y + u * D_param
        y = y * _silu(z)
        out = y @ out_proj_w.T + out_proj_b
        return residual + out

    def _L1_ffn_ref(x, gate_w, experts_gate_up, experts_down, shared_gate_w, shared_up_w, shared_down_w, shared_expert_gate_w):
        import jax, jax.numpy as jnp
        import numpy as np
        HIDDEN_SIZE = 256
        NUM_EXPERTS = 8
        MOE_INTERMEDIATE_SIZE = 352
        NUM_EXPERTS_PER_TOK = 2
        SHARED_EXPERT_INTERMEDIATE_SIZE = 704
        B, T = (2, 256)
        W_SCALE = 0.02
        Bx, Tx, H = x.shape
        E = gate_w.shape[0]
        I = experts_down.shape[2]
        x_flat = x.reshape(Bx * Tx, H)
        logits = x_flat @ gate_w.T
        scores = jax.nn.softmax(logits, axis=-1)
        _, topk_ids = jax.lax.top_k(scores, NUM_EXPERTS_PER_TOK)
        in_topk = jax.nn.one_hot(topk_ids, E, dtype=x.dtype).sum(axis=1)
        w = scores * in_topk
        gu = jnp.einsum('nh,eih->nei', x_flat, experts_gate_up)
        g, u = (gu[..., :I], gu[..., I:])
        h = jax.nn.silu(g) * u
        expert_out = jnp.einsum('nei,ehi->neh', h, experts_down)
        out = jnp.einsum('neh,ne->nh', expert_out, w)
        shared = jax.nn.silu(x_flat @ shared_gate_w.T) * (x_flat @ shared_up_w.T) @ shared_down_w.T
        shared_weight = jax.nn.sigmoid(x_flat @ shared_expert_gate_w.T)
        out = out + shared_weight * shared
        return out.reshape(Bx, Tx, H)
    x = L0_attn_x
    x = x + _L0_attn_ref(_layernorm(x, axis=-1), L0_attn_w_lhs, L0_attn_w_rhs)
    x = x + _L0_ffn_ref(_layernorm(x, axis=-1), L0_ffn_kernel, L0_ffn_input_scale, L0_ffn_kernel_scale, L0_ffn_bias)
    x = x + _L1_attn_ref(_layernorm(x, axis=-1), L1_attn_norm_w, L1_attn_norm_b, L1_attn_in_proj_w, L1_attn_in_proj_b, L1_attn_conv_w, L1_attn_conv_b, L1_attn_x_proj_w, L1_attn_x_proj_b, L1_attn_dt_proj_w, L1_attn_dt_proj_b, L1_attn_A_log, L1_attn_D_param, L1_attn_out_proj_w, L1_attn_out_proj_b)
    x = x + _L1_ffn_ref(_layernorm(x, axis=-1), L1_ffn_gate_w, L1_ffn_experts_gate_up, L1_ffn_experts_down, L1_ffn_shared_gate_w, L1_ffn_shared_up_w, L1_ffn_shared_down_w, L1_ffn_shared_expert_gate_w)
    return x

_drawn_inputs = setup_inputs


def setup_inputs(seed=0):
    import zlib

    import numpy as np

    out = dict(_drawn_inputs(seed))
    spreads = {'L1_attn_norm_w': (1.0, 0.2),
     'L1_attn_norm_b': (0.0, 0.1),
     'L1_attn_in_proj_b': (0.0, 0.1),
     'L1_attn_conv_b': (0.0, 0.1),
     'L1_attn_x_proj_b': (0.0, 0.1),
     'L1_attn_dt_proj_b': (0.0, 0.1),
     'L1_attn_D_param': (1.0, 0.2),
     'L1_attn_out_proj_b': (0.0, 0.1)}
    factors = {}
    for name, (base, spread) in spreads.items():
        noise = np.random.default_rng([zlib.crc32(name.encode()), seed]).standard_normal(out[name].shape)
        drawn = base * np.exp(spread * noise) if base else spread * noise
        out[name] = jnp.asarray(drawn.astype(out[name].dtype))
    for name, factor in factors.items():
        out[name] = (out[name] * factor).astype(out[name].dtype)
    return out
```

```python
import concourse.bass as bass
from concourse import mybir
from contextlib import ExitStack

NB, T, D = 16, 512, 256
P = 128
TT = T // P
DC = D // P
DI = 512
MC = DI // P
NS = 16
TAPS = 4
E, I, SI = 8, 352, 704
NT = NB * TT
SLOTS_T = NT * 2 + E
EPS = 1e-5
UNITS = NS * MC

fp32 = mybir.dt.float32
bf16 = mybir.dt.bfloat16
i32 = mybir.dt.int32
u32 = mybir.dt.uint32
ALU = mybir.AluOpType
ACT = mybir.ActivationFunctionType
AX = mybir.AxisListType


class Banks:

    def __init__(self, tensors, full):
        self.tensors, self.full = tensors, full
        self.fills, self.last = [0] * len(full), [None] * len(full)
        self.uses = {}

    def add(self, name, bank, *readers):
        self.uses[name] = (bank, self.fills[bank], self.last[bank], readers)
        self.fills[bank] += 1
        self.last[bank] = name

    def may_fill(self, eng, name, b, done, before):
        bank, _, last, _ = self.uses[name]
        if last:
            for sem, i in self.uses[last][3]:
                done(eng, sem, b, i)
        else:
            for sem, _ in self.uses[self.last[bank]][3]:
                before(eng, sem, b)

    def filled(self, eng, name, b):
        bank, fills = self.uses[name][:2]
        eng.wait_ge(self.full[bank], b * self.fills[bank] + 2 + fills)

    def fill_sem(self, name):
        return self.full[self.uses[name][0]]

    def __getitem__(self, name):
        return self.tensors[self.uses[name][0]]


def build(nc, a, out):
    x3_d = nc.dram_tensor("x3_scratch", (NB * T, D), fp32, kind="Internal").ap()
    x4_d = nc.dram_tensor("x4_scratch", (NB * T, D), fp32, kind="Internal").ap()
    bd = nc.dram_tensor("b_scratch", (NB * NS, T), fp32, kind="Internal").ap()
    xs_d = nc.dram_tensor("slots_in", (SLOTS_T * P, D), fp32, kind="Internal").ap()
    ys_d = nc.dram_tensor("slots_out", (SLOTS_T * P, D), fp32, kind="Internal").ap()

    top = ExitStack()
    with top:
        def psb(name, shape, dt=fp32):
            return top.enter_context(nc.sbuf_tensor(name, shape, dt))

        taken = []

        def sem(name):
            taken.append(nc.alloc_semaphore(name=name))
            return taken[-1]

        ident = psb("ident", [P, P])
        identb = psb("identb", [P, P], bf16)
        oh = psb("oh", [P, 2, NT, E])
        topw = psb("topw", [P, NT, 2])
        sharew = psb("sharew", [P, NT])
        banks = [top.enter_context(nc.psum_tensor(f"bank{k}", [P, 512], fp32)) for k in range(8)]
        layers(nc, sem, a, ident, identb, oh, topw, sharew, banks, x3_d, x4_d, bd, xs_d)
        nc.clear_and_free_semaphores(taken)
        nc.all_engine_barrier()
        experts(nc, sem, a, out, ident, oh, topw, sharew, banks, x3_d, x4_d, xs_d, ys_d)


def layers(nc, sem, a, ident, identb, oh, topw, sharew, banks, x3_d, x4_d, bd, xs_d):
    ctx = ExitStack()
    with ctx:
        def sb(name, shape, dt=fp32):
            return ctx.enter_context(nc.sbuf_tensor(name, shape, dt))

        w_in = sb("w_in", [P, DC, 2 * DI])
        w_dt = sb("w_dt", [P, MC, DI])
        w_x = sb("w_x", [P, MC, 2 * NS])
        w_out = sb("w_out", [P, MC, D])
        w_gate = sb("w_gate", [P, DC, E + 1])
        kern = sb("kern", [P, DC, D], bf16)
        kq = sb("kq", [P, DC, D], bf16)
        wl, wr = sb("wl", [P, DC]), sb("wr", [P, DC])
        s_in, s_k = sb("s_in", [P, 1]), sb("s_k", [P, 1])
        rs_in, rs_k, s_both = sb("rs_in", [P, 1]), sb("rs_k", [P, 1]), sb("s_both", [P, 1])
        fbias = sb("fbias", [P, D], bf16)
        nw, nb_ = sb("nw", [P, DC]), sb("nb_", [P, DC])
        in_b, in_bh = sb("in_b", [P, 2 * MC]), sb("in_bh", [P, 2 * MC])
        cw, cb = sb("cw", [P, MC, TAPS]), sb("cb", [P, MC])
        cwh, cbh = sb("cwh", [P, MC, TAPS]), sb("cbh", [P, MC])
        xb_b, xb_c = sb("xb_b", [NS, 1]), sb("xb_c", [P, NS])
        dt_b, dpar = sb("dt_b", [P, MC]), sb("dpar", [P, MC])
        alog, amat = sb("alog", [P, MC, NS]), sb("amat", [P, MC, NS])
        out_b = sb("out_b", [P, D])
        half, eps = sb("half", [P, TT]), sb("eps", [P, TT])
        iota8 = sb("iota8", [P, E])
        zero = sb("zero", [P, 512])

        x = sb("x", [P, TT, D])
        xn = sb("xn", [P, TT, D])
        st = sb("st", [P, TT, 6])
        mv = sb("mv", [P, 4, TT, 2])
        ve = sb("ve", [P, 4, TT])
        rstd = sb("rstd", [P, 4, TT])
        r34 = sb("r34", [P, TT])
        xl, xr = sb("xl", [P, DC, T]), sb("xr", [P, DC, T])
        nmax, rsum, rinv = sb("nmax", [P, TT]), sb("rsum", [P, TT]), sb("rinv", [P, TT])
        prob = sb("prob", [P, TT, T])
        xc = sb("xc", [P, MC, TAPS - 1 + T])
        probT = xc[:, :, TAPS - 1:]
        x1 = sb("x1", [P, TT, D])
        xb = sb("xb", [P, TT, D], bf16)
        pf = prob[:, :, :].rearrange("p t n -> p (t n)")
        qs, qm = (pf[:, k * TT * D:(k + 1) * TT * D].rearrange("p (t d) -> p t d", t=TT) for k in range(2))
        qb = sb("qb", [P, TT, D], bf16)
        qT = sb("qT", [P, DC, T], bf16)
        yb, yb2 = sb("yb", [P, TT, D], bf16), sb("yb2", [P, TT, D], bf16)
        x2 = sb("x2", [P, TT, D])
        res = sb("res", [P, TT, D])
        base3 = sb("base3", [P, TT, D])
        r4, r4T = xn, xl
        zs, zt = sb("zs", [P, MC, T]), prob
        ch, ct = sb("ch", [P, 2, T]), sb("ct", [P, 2, T])
        u = sb("u", [P, MC, T])
        sp = sb("sp", [P, 2, T])
        delta, du = sb("delta", [P, MC, T]), sb("du", [P, MC, T])
        bs = sb("bs", [NS, T])
        cT = sb("cT", [P, TT, NS])
        bbc = sb("bbc", [P, 4, T])
        dbu = sb("dbu", [P, 4, T])
        h = sb("h", [P, 2, MC, T])
        acc = sb("acc", [P, TT, DI])
        y2, y3 = sb("y2", [P, 2, T]), h[:, 0]
        x3 = base3
        x4 = sb("x4", [P, TT, D])
        x4T = acc
        lg = sb("lg", [P, TT, E + 1])
        lmax, lsum, lrec = sb("lmax", [P, TT]), sb("lsum", [P, TT]), sb("lrec", [P, TT])
        lsub, lexp, score = sb("lsub", [P, TT, E]), sb("lexp", [P, TT, E]), sb("score", [P, TT, E])
        m8 = sb("m8", [P, TT, E])
        i8, f8 = sb("i8", [P, TT, E], u32), sb("f8", [P, TT, E])
        ohb = sb("ohb", [P, 2, TT, E])
        sg, sg1, sg2 = sb("sg", [P, TT]), sb("sg1", [P, TT]), sb("sg2", [P, TT])

        sems = {}
        SHARED = {"norm_stats": ["stats1", "stats2", "stats3"], "norm_mv": ["mv1", "mv2", "mv3"],
                  "norm_ve": ["ve1", "ve2", "ve3"], "norm_rstd": ["rstd1", "rstd2", "rstd3"],
                  "inner_step": ["sq4", "mul4", "ve4", "rstd4"],
                  "q_step": ["q_scaled", "q_expo", "q_magic", "q_added", "q_rounded", "q_nan"],
                  "router_step": ["lg_ready", "lmax_ready", "lsub_ready", "lsum_ready", "lrec_ready", "score_ready", "max_ready",
                                  "idx_ready", "idxf_ready", "oh_ready", "sg1_ready", "sg2_ready"]}
        PLACE = {step: (group, i) for group, steps in SHARED.items() for i, step in enumerate(steps)}

        def S(name):
            name = PLACE.get(name, (name,))[0]
            if name not in sems:
                sems[name] = sem(name)
            return sems[name]

        PER = dict(x_loaded=1, stats5=1, mv5=1,
                   ve5=1, rstd5=1,
                   xn_ready=1, xl_ready=DC, xr_ready=DC, neg_max=TT, prob_ready=TT, inv_ready=1, probT_ready=TT,
                   x1_ready=2, xb_ready=1, 
                   q_ready=1, qT_ready=1, yb_ready=2, yb2_ready=1, x2_ready=1, 
                   res_ready=1, base_a=1, base_ready=1, r4_ready=1, r4T_ready=DC,
                   xc_ready=MC, zh_ready=MC, zt_ready=MC, zs_ready=MC, conv_tap=MC * (TAPS - 1), conv_ready=MC,
                   conv_tanh=MC, u_ready=MC, dt_min=MC, dt_exp=MC, dt_ln=MC, delta_ready=MC, du_ready=MC,
                   bs_ready=1, b_stored=1, cT_ready=1, b_row0=4, b_row1=4, b_row2=4, b_row3=4,
                   da_ready=UNITS, dbu_ready=UNITS, scan_done=UNITS, acc_ready=NS * TT,
                   y2_ready=MC, y3_ready=MC, projected=1, x3_ready=2, x3_stored=1, x4_ready=1, x4_stored=1, x4T_ready=DC,
                   lexp_ready=1, 
                   sg_ready=1, 
                   routed=1,
                   **{group: len(steps) for group, steps in SHARED.items()})
        UNIT = {"x_loaded": 16, "b_stored": 16, "b_row0": 16, "b_row1": 16, "b_row2": 16, "b_row3": 16,
                "x3_stored": 16, "x4_stored": 16}

        def done(eng, name, b, i=None):
            name, i = PLACE.get(name, (name, i))
            n, k = PER[name], UNIT.get(name, 1)
            i = n - 1 if i is None else i
            eng.wait_ge(S(name), b * (n * k) + k * (2 + i))

        def before(eng, name, b, i=0):
            name = PLACE.get(name, (name,))[0]
            n, k = PER[name], UNIT.get(name, 1)
            eng.wait_ge(S(name), b * (n * k) + k * (1 + i))

        front = Banks(banks[0:4], [sem(f"front_full{k}") for k in range(4)])
        back = Banks(banks[4:6], [sem(f"back_full{k}") for k in range(2)])
        order = [(f"xT{c}", ("xr_ready", c)) for c in range(DC)]
        order += [(f"score{i}", ("neg_max", i), ("prob_ready", i)) for i in range(TT)]
        order += [(f"probT{t}", ("probT_ready", t)) for t in range(TT)] + [(f"av{k}", ("x1_ready", k)) for k in range(2)]
        order += [("qT", ("qT_ready", 0))] + [(f"ffn{k}", ("yb_ready", k)) for k in range(2)]
        order += [(f"r4T{c}", ("r4T_ready", c)) for c in range(DC)] + [(f"in{m}", ("xc_ready", m)) for m in range(MC)]
        order += [(f"in{MC + m}", ("zt_ready", m)) for m in range(MC)] + [("xB", ("bs_ready", 0)), ("xC", ("cT_ready", 0))]
        order += [(f"dt{m}", ("delta_ready", m)) for m in range(MC)]
        for n, (name, *readers) in enumerate(order):
            front.add(name, n % 4, *readers)
        order = [(f"hT{s}.{t}", ("acc_ready", s * TT + t)) for s in range(NS) for t in range(TT)]
        order += [(f"yT{m}", ("y2_ready", m)) for m in range(MC)] + [(f"out{k}", ("x3_ready", k)) for k in range(2)]
        order += [(f"x4T{c}", ("x4T_ready", c)) for c in range(DC)] + [("logit", ("lg_ready", 0))]
        for n, (name, *readers) in enumerate(order):
            back.add(name, n % 2, *readers)

        def db(n):
            return banks[6 + n % 2]

        w_loaded, a_loaded, zero_ready, xs_zeroed = sem("w_loaded"), sem("a_loaded"), sem("zero_ready"), sem("xs_zeroed")
        waited = sem("waited")
        id_zero, id_ready, iota_ready = sem("id_zero"), sem("id_ready"), sem("iota_ready")
        consts, kq_chain, amat_ready = sem("consts"), sem("kq_chain"), sem("amat_ready")

        small = [(wl, a["w_lhs"]), (wr, a["w_rhs"]), (s_in, a["s_in"].partition_broadcast(P)),
                 (s_k, a["s_k"].partition_broadcast(P)), (fbias, a["fbias"].partition_broadcast(P)), (nw, a["norm_w"]),
                 (nb_, a["norm_b"]), (in_b, a["in_b"]), (cw, a["conv_w"].rearrange("(m p) a k -> p m (a k)", p=P)),
                 (cb, a["conv_b"]), (xb_b, a["x_bb"]), (xb_c, a["x_bc"].partition_broadcast(P)),
                 (dt_b, a["dt_b"]), (dpar, a["d_param"]), (alog, a["a_log"].rearrange("(m p) s -> p m s", p=P)),
                 (out_b, a["out_b"].partition_broadcast(P)), (kern, a["kernel"].rearrange("(c p) n -> p c n", p=P))]
        large = [(w_in, a["w_in"].rearrange("(c p) n -> p c n", p=P)), (w_dt, a["w_dt"].rearrange("(c p) n -> p c n", p=P)),
                 (w_x, a["w_x"].rearrange("(c p) n -> p c n", p=P)), (w_out, a["w_out"].rearrange("(c p) n -> p c n", p=P)),
                 (w_gate, a["w_gate"].rearrange("(c p) n -> p c n", p=P))]

        def ap(t):
            return t if isinstance(t, bass.AP) else t[tuple(slice(None) for _ in t.shape)]

        def start_at_one(eng, names, bank_sems=()):
            for name in names:
                eng.sem_inc(S(name), UNIT.get(name, 1))
            for s in bank_sems:
                eng.sem_inc(s, 1)

        block = ctx.enter_context(nc.Block())

        @block.sync
        def _(sp_):
            start_at_one(sp_, list(PER), front.full + back.full)
            for t, src in small:
                sp_.dma_start(ap(t), src).then_inc(a_loaded, 16)
            for t, src in large:
                sp_.dma_start(ap(t), src).then_inc(w_loaded, 16)
            sp_.wait_ge(zero_ready, 1)
            xs_v = xs_d.rearrange("(g p) d -> p g d", p=P)
            for g in range(0, SLOTS_T, 2):
                sp_.dma_start(xs_v[:, g:g + 2, :], zero[:, :].rearrange("p (g d) -> p g d", g=2)).then_inc(xs_zeroed, 16)
            x_v = a["x"].rearrange("b (j p) d -> p (b j) d", p=P)
            with sp_.Fori(0, NB) as b:
                before(sp_, "x1_ready", b)
                sp_.dma_start(x[:, :, :], x_v[:, bass.ds(b * TT, TT), :]).then_inc(S("x_loaded"), 16)
                done(sp_, "bs_ready", b)
                sp_.dma_start(bd[bass.ds(b * NS, NS), :], bs[:, :]).then_inc(S("b_stored"), 16)
                done(sp_, "b_stored", b)
                for s in range(NS):
                    before(sp_, "dbu_ready", b, max(0, (s - 3) * MC))
                    sp_.dma_start(bbc[:, s % 4, :], bd[bass.ds(b * NS + s, 1), :].rearrange("a t -> (a t)").partition_broadcast(P))\
                        .then_inc(S(f"b_row{s % 4}"), 16)
                done(sp_, "x3_ready", b)
                sp_.dma_start(x3_d.rearrange("(g p) d -> p g d", p=P)[:, bass.ds(b * TT, TT), :], x3[:, :, :]).then_inc(S("x3_stored"), 16)
                done(sp_, "x4_ready", b)
                sp_.dma_start(x4_d.rearrange("(g p) d -> p g d", p=P)[:, bass.ds(b * TT, TT), :], x4[:, :, :]).then_inc(S("x4_stored"), 16)
            sp_.wait_ge(S("x3_stored"), 16 * (NB + 1))
            sp_.wait_ge(S("x4_stored"), 16 * (NB + 1))
            sp_.wait_ge(xs_zeroed, 16 * (SLOTS_T // 2))

        @block.gpsimd
        def _(pool):
            g = nc.gpsimd
            g.memset(zero[:, :], 0.0).then_inc(zero_ready, 1)
            g.memset(half[:, :], -0.5).then_inc(zero_ready, 1)
            g.memset(eps[:, :], EPS).then_inc(zero_ready, 1)
            g.memset(ident[:, :], 0.0).then_inc(id_zero, 1)
            g.memset(identb[:, :], 0.0).then_inc(id_zero, 1)
            g.memset(xc[:, :, 0:TAPS - 1], 0.0).then_inc(zero_ready, 1)
            pool.wait_ge(id_zero, 2)
            for m in (ident, identb):
                g.affine_select(out=m[:, :], in_=m[:, :], compare_op=ALU.not_equal, fill=1.0, base=0,
                                pattern=[[-1, P]], channel_multiplier=1).then_inc(id_ready, 1)
            g.iota(iota8[:, :], pattern=[[1, E]], base=0, channel_multiplier=0,
                   allow_small_or_imprecise_dtypes=True).then_inc(iota_ready, 1)

            def rstd_of(b, n, mvn):
                done(pool, f"mv{n}", b)
                g.tensor_tensor(ve[:, mvn, :], mv[:, mvn, :, 1], eps[:, :], ALU.add).then_inc(S(f"ve{n}"), 1)
                done(pool, f"ve{n}", b)
                g.tensor_tensor(rstd[:, mvn, :], ve[:, mvn, :], half[:, :], ALU.pow).then_inc(S(f"rstd{n}"), 1)

            with pool.Fori(0, NB) as b:
                rstd_of(b, 1, 0)
                rstd_of(b, 2, 1)
                done(pool, "q_rounded", b)
                done(pool, "q_nan", b)
                g.tensor_tensor(qb[:, :, :], qm[:, :, :], qs[:, :, :], ALU.add).then_inc(S("q_ready"), 1)
                rstd_of(b, 3, 2)
                done(pool, "rstd3", b)
                g.tensor_tensor(r34[:, :], rstd[:, 2, :], rstd[:, 2, :], ALU.mult).then_inc(S("sq4"), 1)
                done(pool, "sq4", b)
                g.tensor_tensor(r34[:, :], r34[:, :], mv[:, 2, :, 1], ALU.mult).then_inc(S("mul4"), 1)
                done(pool, "mul4", b)
                g.tensor_tensor(r34[:, :], r34[:, :], eps[:, :], ALU.add).then_inc(S("ve4"), 1)
                done(pool, "ve4", b)
                g.tensor_tensor(r34[:, :], r34[:, :], half[:, :], ALU.pow).then_inc(S("rstd4"), 1)
                done(pool, "x2_ready", b)
                before(pool, "x3_ready", b)
                for j in range(TT):
                    last = g.tensor_tensor(base3[:, j, :], x2[:, j, :], out_b[:, :], ALU.add)
                last.then_inc(S("base_a"), 1)
                done(pool, "base_a", b)
                done(pool, "res_ready", b)
                g.tensor_tensor(base3[:, :, :], base3[:, :, :], res[:, :, :], ALU.add).then_inc(S("base_ready"), 1)
                for m in range(MC):
                    done(pool, "delta_ready", b, m)
                    g.tensor_tensor(du[:, m, :], delta[:, m, :], u[:, m, :], ALU.mult).then_inc(S("du_ready"), 1)
                done(pool, "du_ready", b)
                for n in range(UNITS):
                    s, m = divmod(n, MC)
                    if m == 0:
                        done(pool, f"b_row{s % 4}", b, s // 4)
                    before(pool, "scan_done", b, max(0, n - 3))
                    g.tensor_tensor(dbu[:, n % 4, :], du[:, m, :], bbc[:, s % 4, :], ALU.mult).then_inc(S("dbu_ready"), 1)
                rstd_of(b, 5, 3)

        @block.scalar
        def _(act):
            f = nc.scalar.activation
            act.wait_ge(a_loaded, 16 * len(small))
            act.wait_ge(w_loaded, 16 * len(large))
            f(amat[:, :, :], alog[:, :, :], ACT.Exp).then_inc(consts, 1)
            with act.Fori(0, NB) as b:
                for c in range(DC):
                    front.filled(act, f"xT{c}", b)
                    f(xl[:, c, :], front[f"xT{c}"][:, :], ACT.Copy, scale=wl[:, c:c + 1]).then_inc(S("xl_ready"), 1)
                    f(xr[:, c, :], front[f"xT{c}"][:, :], ACT.Copy, scale=wr[:, c:c + 1]).then_inc(S("xr_ready"), 1)
                for i in range(TT):
                    done(act, "neg_max", b, i)
                    f(prob[:, i, :], front[f"score{i}"][:, :], ACT.Exp, bias=nmax[:, i:i + 1],
                      accum_out=rsum[:, i:i + 1]).then_inc(S("prob_ready"), 1)
                for t in range(TT):
                    front.filled(act, f"probT{t}", b)
                    f(probT[:, t, :], front[f"probT{t}"][:, :], ACT.Copy).then_inc(S("probT_ready"), 1)
                front.filled(act, "qT", b)
                qp = front["qT"][:, :].bitcast(bf16)
                f(qT[:, :, :], qp.rearrange("p (c t) -> p c t", c=DC), ACT.Copy).then_inc(S("qT_ready"), 1)
                for k in range(2):
                    front.filled(act, f"ffn{k}", b)
                    f(yb[:, 2 * k:2 * k + 2, :], front[f"ffn{k}"][:, :].rearrange("p (j d) -> p j d", j=2), ACT.Copy,
                      scale=s_both[:, 0:1]).then_inc(S("yb_ready"), 1)
                for c in range(DC):
                    front.filled(act, f"r4T{c}", b)
                    f(r4T[:, c, :], front[f"r4T{c}"][:, :], ACT.Identity, bias=nb_[:, c:c + 1],
                      scale=nw[:, c:c + 1]).then_inc(S("r4T_ready"), 1)
                for m in range(MC):
                    front.filled(act, f"in{m}", b)
                    f(xc[:, m, TAPS - 1:], front[f"in{m}"][:, :], ACT.Identity, bias=in_b[:, m:m + 1]).then_inc(S("xc_ready"), 1)
                for m in range(MC):
                    front.filled(act, f"in{MC + m}", b)
                    f(zs[:, m, :], front[f"in{MC + m}"][:, :], ACT.Identity, bias=in_bh[:, MC + m:MC + m + 1], scale=0.5).then_inc(S("zh_ready"), 1)
                    f(zt[:, m, :], front[f"in{MC + m}"][:, :], ACT.Tanh, bias=in_bh[:, MC + m:MC + m + 1], scale=0.5).then_inc(S("zt_ready"), 1)
                for m in range(MC):
                    done(act, "conv_ready", b, m)
                    f(ct[:, m % 2, :], ch[:, m % 2, :], ACT.Tanh).then_inc(S("conv_tanh"), 1)
                front.filled(act, "xB", b)
                before(act, "b_stored", b)
                f(bs[:, :], front["xB"][0:NS, :], ACT.Identity, bias=xb_b[:, 0:1]).then_inc(S("bs_ready"), 1)
                for m in range(MC):
                    done(act, "dt_min", b, m)
                    f(sp[:, m % 2, :], sp[:, m % 2, :], ACT.Exp).then_inc(S("dt_exp"), 1)
                    done(act, "dt_exp", b, m)
                    f(sp[:, m % 2, :], sp[:, m % 2, :], ACT.Ln, bias=1.0).then_inc(S("dt_ln"), 1)
                for n in range(UNITS):
                    s, m = divmod(n, MC)
                    if n < MC:
                        done(act, "delta_ready", b, m)
                    before(act, "scan_done", b, max(0, n - 1))
                    f(db(n)[:, :], delta[:, m, :], ACT.Exp, scale=amat[:, m, s:s + 1]).then_inc(S("da_ready"), 1)
                for c in range(DC):
                    back.filled(act, f"x4T{c}", b)
                    f(x4T[:, c, :], back[f"x4T{c}"][:, :], ACT.Copy).then_inc(S("x4T_ready"), 1)
                done(act, "lsub_ready", b)
                f(lexp[:, :, :], lsub[:, :, :], ACT.Exp).then_inc(S("lexp_ready"), 1)
                f(sg[:, :], lg[:, :, E], ACT.Exp, scale=-1.0).then_inc(S("sg_ready"), 1)

        @block.vector
        def _(dve):
            v = nc.vector
            dve.wait_ge(a_loaded, 16 * len(small))
            dve.wait_ge(consts, 1)
            v.tensor_scalar(amat[:, :, :], amat[:, :, :], -1.0, None, ALU.mult).then_inc(amat_ready, 1)
            v.tensor_scalar(in_bh[:, :], in_b[:, :], 0.5, None, ALU.mult).then_inc(amat_ready, 1)
            v.tensor_scalar(cwh[:, :, :], cw[:, :, :], 0.5, None, ALU.mult)
            v.tensor_scalar(cbh[:, :], cb[:, :], 0.5, None, ALU.mult)
            v.tensor_tensor(s_both[:, :], s_in[:, :], s_k[:, :], ALU.mult)
            v.reciprocal(rs_in[:, :], s_in[:, :])
            v.reciprocal(rs_k[:, :], s_k[:, :]).then_inc(amat_ready, 1)
            dve.wait_ge(amat_ready, 3)

            def to_e4m3(x_in, scale, q, m, wait, e_sem):
                v.tensor_scalar(q, x_in, scale, None, ALU.mult).then_inc(e_sem[0], 1)
                wait(0)
                v.tensor_scalar(m.bitcast(i32), q.bitcast(i32), 0x7F800000, None, ALU.bitwise_and).then_inc(e_sem[1], 1)
                wait(1)
                v.tensor_scalar(m, m, 2.0 ** -6, 1.5 * 2.0 ** 20, ALU.max, ALU.mult).then_inc(e_sem[2], 1)
                wait(2)
                v.tensor_tensor(q, q, m, ALU.add).then_inc(e_sem[3], 1)
                wait(3)
                v.tensor_tensor(m, q, m, ALU.subtract).then_inc(e_sem[4], 1)
                wait(4)
                v.tensor_scalar(q, m, 3.4e38 / 460.0, 0.0, ALU.mult, ALU.mult).then_inc(e_sem[5], 1)

            kq_q, kq_m = qs[:, 0:DC, :], qm[:, 0:DC, :]
            to_e4m3(kern[:, :, :], rs_k[:, 0:1], kq_q, kq_m, lambda n: dve.wait_ge(kq_chain, n + 1), [kq_chain] * 6)
            dve.wait_ge(kq_chain, 6)
            v.tensor_tensor(kq[:, :, :], kq_m, kq_q, ALU.add).then_inc(kq_chain, 1)
            dve.wait_ge(kq_chain, 7)
            dve.wait_ge(zero_ready, 4)
            dve.wait_ge(iota_ready, 1)

            def stats(b, n, mvn, src):
                for j in range(TT):
                    last = v.bn_stats(st[:, j, :], src[:, j, :])
                last.then_inc(S(f"stats{n}"), 1)
                done(dve, f"stats{n}", b)
                dve.sem_inc(waited, 1)
                for j in range(TT):
                    last = v.bn_aggr(mv[:, mvn, j, :], st[:, j, :])
                last.then_inc(S(f"mv{n}"), 1)

            def normed(b, n, mvn, src, dst, name):
                done(dve, f"rstd{n}", b)
                for j in range(TT):
                    last = v.tensor_scalar(dst[:, j, :], src[:, j, :], mv[:, mvn, j, 0:1], rstd[:, mvn, j:j + 1],
                                           ALU.subtract, ALU.mult)
                last.then_inc(S(name), 1)

            with dve.Fori(0, NB) as b:
                done(dve, "x_loaded", b)
                stats(b, 1, 0, x)
                normed(b, 1, 0, x, xn, "xn_ready")
                for i in range(TT):
                    front.filled(dve, f"score{i}", b)
                    v.tensor_reduce(nmax[:, i:i + 1], front[f"score{i}"][:, :], AX.X, ALU.max, negate=True).then_inc(S("neg_max"), 1)
                done(dve, "prob_ready", b)
                v.reciprocal(rinv[:, :], rsum[:, :]).then_inc(S("inv_ready"), 1)
                done(dve, "inv_ready", b)
                for k in range(2):
                    front.filled(dve, f"av{k}", b)
                    for i in (2 * k, 2 * k + 1):
                        last = v.scalar_tensor_tensor(x1[:, i, :], front[f"av{k}"][:, (i % 2) * D:(i % 2 + 1) * D], rinv[:, i:i + 1],
                                                      x[:, i, :], ALU.mult, ALU.add)
                    last.then_inc(S("x1_ready"), 1)
                done(dve, "x1_ready", b)
                stats(b, 2, 1, x1)
                normed(b, 2, 1, x1, xb, "xb_ready")
                done(dve, "xb_ready", b)
                names = ["q_scaled", "q_expo", "q_magic", "q_added", "q_rounded", "q_nan"]
                to_e4m3(xb[:, :, :], rs_in[:, 0:1], qs[:, :, :], qm[:, :, :], lambda n: done(dve, names[n], b), [S(n) for n in names])
                done(dve, "yb_ready", b)
                for j in range(TT):
                    last = v.tensor_tensor(yb2[:, j, :], yb[:, j, :], fbias[:, :], ALU.add)
                last.then_inc(S("yb2_ready"), 1)
                done(dve, "yb2_ready", b)
                v.tensor_tensor(x2[:, :, :], x1[:, :, :], yb2[:, :, :], ALU.add).then_inc(S("x2_ready"), 1)
                done(dve, "x2_ready", b)
                stats(b, 3, 2, x2)
                normed(b, 3, 2, x2, res, "res_ready")
                done(dve, "res_ready", b)
                done(dve, "rstd4", b)
                for j in range(TT):
                    last = v.tensor_scalar(r4[:, j, :], res[:, j, :], r34[:, j:j + 1], None, ALU.mult)
                last.then_inc(S("r4_ready"), 1)
                for m in range(MC):
                    done(dve, "xc_ready", b, m)
                    if m >= 2:
                        done(dve, "u_ready", b, m - 2)
                    v.tensor_scalar(ch[:, m % 2, :], xc[:, m, 0:T], cwh[:, m, 0:1], cbh[:, m:m + 1], ALU.mult, ALU.add).then_inc(S("conv_tap"), 1)
                    for k in range(1, TAPS):
                        done(dve, "conv_tap", b, 3 * m + k - 1)
                        v.scalar_tensor_tensor(ch[:, m % 2, :], xc[:, m, k:k + T], cwh[:, m, k:k + 1], ch[:, m % 2, :],
                                               ALU.mult, ALU.add).then_inc(S("conv_tap" if k < TAPS - 1 else "conv_ready"), 1)
                    done(dve, "conv_tanh", b, m)
                    v.scalar_tensor_tensor(u[:, m, :], ct[:, m % 2, :], 1.0, ch[:, m % 2, :], ALU.add, ALU.mult).then_inc(S("u_ready"), 1)
                    done(dve, "zt_ready", b, m)
                    v.scalar_tensor_tensor(zs[:, m, :], zt[:, m, :], 1.0, zs[:, m, :], ALU.add, ALU.mult).then_inc(S("zs_ready"), 1)
                front.filled(dve, "xC", b)
                v.tensor_tensor(cT[:, :, :], front["xC"][:, 0:TT * NS].rearrange("p (t s) -> p t s", s=NS),
                                xb_c[:, :].unsqueeze(1).broadcast_to([P, TT, NS]), ALU.add).then_inc(S("cT_ready"), 1)
                done(dve, "cT_ready", b)
                for m in range(MC + 2):
                    if m >= 2:
                        k = m - 2
                        done(dve, "dt_ln", b, k)
                        v.scalar_tensor_tensor(delta[:, k, :], front[f"dt{k}"][:, :], dt_b[:, k:k + 1], sp[:, k % 2, :],
                                               ALU.add, ALU.max).then_inc(S("delta_ready"), 1)
                    if m < MC:
                        if m >= 2:
                            done(dve, "delta_ready", b, m - 2)
                        front.filled(dve, f"dt{m}", b)
                        v.tensor_scalar(sp[:, m % 2, :], front[f"dt{m}"][:, :], dt_b[:, m:m + 1], 40.0, ALU.add, ALU.min).then_inc(S("dt_min"), 1)

                def add_state(s, t):
                    back.filled(dve, f"hT{s}.{t}", b)
                    if s == 0:
                        v.tensor_scalar(acc[:, t, :], back[f"hT{s}.{t}"][:, :], cT[:, t, s:s + 1], None, ALU.mult)\
                            .then_inc(S("acc_ready"), 1)
                    else:
                        done(dve, "acc_ready", b, (s - 1) * TT + t)
                        v.scalar_tensor_tensor(acc[:, t, :], back[f"hT{s}.{t}"][:, :], cT[:, t, s:s + 1], acc[:, t, :],
                                               ALU.mult, ALU.add).then_inc(S("acc_ready"), 1)

                for n in range(UNITS):
                    s, m = divmod(n, MC)
                    done(dve, "da_ready", b, n)
                    done(dve, "dbu_ready", b, n)
                    if m == 0 and s >= 2:
                        back.filled(dve, f"hT{s - 2}.{TT - 1}", b)
                    v.tensor_tensor_scan(h[:, s % 2, m, :], db(n)[:, :], dbu[:, n % 4, :], 0.0, ALU.mult, ALU.add)\
                        .then_inc(S("scan_done"), 1)
                    if s > 0:
                        add_state(s - 1, m)
                for t in range(TT):
                    add_state(NS - 1, t)
                for m in range(MC):
                    back.filled(dve, f"yT{m}", b)
                    v.scalar_tensor_tensor(y2[:, m % 2, :], u[:, m, :], dpar[:, m:m + 1], back[f"yT{m}"][:, :], ALU.mult, ALU.add)\
                        .then_inc(S("y2_ready"), 1)
                    done(dve, "y2_ready", b, m)
                    v.tensor_tensor(y3[:, m, :], y2[:, m % 2, :], zs[:, m, :], ALU.mult).then_inc(S("y3_ready"), 1)
                done(dve, "base_ready", b)
                before(dve, "x3_stored", b)
                for k in range(2):
                    back.filled(dve, f"out{k}", b)
                    v.tensor_tensor(x3[:, 2 * k:2 * k + 2, :], back[f"out{k}"][:, :].rearrange("p (j d) -> p j d", j=2),
                                    base3[:, 2 * k:2 * k + 2, :], ALU.add).then_inc(S("x3_ready"), 1)
                done(dve, "x3_ready", b)
                stats(b, 5, 3, x3)
                before(dve, "x4_stored", b)
                normed(b, 5, 3, x3, x4, "x4_ready")
                back.filled(dve, "logit", b)
                v.tensor_copy(lg[:, :, :], back["logit"][:, 0:TT * (E + 1)].rearrange("p (t e) -> p t e", e=E + 1)).then_inc(S("lg_ready"), 1)
                done(dve, "lg_ready", b)
                v.tensor_reduce(lmax[:, :], lg[:, :, 0:E], AX.X, ALU.max).then_inc(S("lmax_ready"), 1)
                done(dve, "lmax_ready", b)
                v.tensor_tensor(lsub[:, :, :], lg[:, :, 0:E], lmax[:, :].unsqueeze(2).broadcast_to([P, TT, E]), ALU.subtract)\
                    .then_inc(S("lsub_ready"), 1)
                done(dve, "lexp_ready", b)
                v.tensor_reduce(lsum[:, :], lexp[:, :, :], AX.X, ALU.add).then_inc(S("lsum_ready"), 1)
                done(dve, "lsum_ready", b)
                v.reciprocal(lrec[:, :], lsum[:, :]).then_inc(S("lrec_ready"), 1)
                done(dve, "lrec_ready", b)
                v.tensor_tensor(score[:, :, :], lexp[:, :, :], lrec[:, :].unsqueeze(2).broadcast_to([P, TT, E]), ALU.mult)\
                    .then_inc(S("score_ready"), 1)
                done(dve, "score_ready", b)
                dve.sem_inc(waited, 1)
                for j in range(TT):
                    last = v.max(m8[:, j, :], score[:, j, :])
                last.then_inc(S("max_ready"), 1)
                done(dve, "max_ready", b)
                dve.sem_inc(waited, 1)
                for j in range(TT):
                    last = v.max_index(i8[:, j, :], m8[:, j, :], score[:, j, :])
                last.then_inc(S("idx_ready"), 1)
                done(dve, "idx_ready", b)
                v.tensor_copy(f8[:, :, :], i8[:, :, :]).then_inc(S("idxf_ready"), 1)
                done(dve, "idxf_ready", b)
                for k in range(2):
                    for j in range(TT):
                        last = v.tensor_scalar(ohb[:, k, j, :], iota8[:, :], f8[:, j, k:k + 1], None, ALU.is_equal)
                last.then_inc(S("oh_ready"), 1)
                done(dve, "oh_ready", b)
                for k in range(2):
                    v.tensor_copy(oh[:, k, bass.ds(b * TT, TT), :], ohb[:, k, :, :])
                v.tensor_copy(topw[:, bass.ds(b * TT, TT), :], m8[:, :, 0:2])
                done(dve, "sg_ready", b)
                v.tensor_scalar(sg1[:, :], sg[:, :], 1.0, None, ALU.add).then_inc(S("sg1_ready"), 1)
                done(dve, "sg1_ready", b)
                v.reciprocal(sg2[:, :], sg1[:, :]).then_inc(S("sg2_ready"), 1)
                done(dve, "sg2_ready", b)
                v.tensor_copy(sharew[:, bass.ds(b * TT, TT)], sg2[:, :]).then_inc(S("routed"), 1)

        @block.tensor
        def _(pe):
            mm, tr = nc.tensor.matmul, nc.tensor.transpose
            pe.wait_ge(id_ready, 2)
            pe.wait_ge(kq_chain, 7)
            pe.wait_ge(w_loaded, 16 * len(large))
            with pe.Fori(0, NB) as b:
                done(pe, "xn_ready", b)
                for c in range(DC):
                    front.may_fill(pe, f"xT{c}", b, done, before)
                    for j in range(TT):
                        last = tr(front[f"xT{c}"][:, j * P:(j + 1) * P], xn[:, j, c * P:(c + 1) * P], ident[:, :])
                    last.then_inc(front.fill_sem(f"xT{c}"), 1)
                done(pe, "xl_ready", b)
                done(pe, "xr_ready", b)
                for i in range(TT):
                    front.may_fill(pe, f"score{i}", b, done, before)
                    for c in range(DC):
                        last = mm(front[f"score{i}"][:, :], xl[:, c, i * P:(i + 1) * P], xr[:, c, :], start=c == 0, stop=c == DC - 1)
                    last.then_inc(front.fill_sem(f"score{i}"), 1)
                done(pe, "prob_ready", b)
                for t in range(TT):
                    front.may_fill(pe, f"probT{t}", b, done, before)
                    for i in range(TT):
                        last = tr(front[f"probT{t}"][:, i * P:(i + 1) * P], prob[:, i, t * P:(t + 1) * P], ident[:, :])
                    last.then_inc(front.fill_sem(f"probT{t}"), 1)
                done(pe, "probT_ready", b)
                for k in range(2):
                    front.may_fill(pe, f"av{k}", b, done, before)
                    for i in (2 * k, 2 * k + 1):
                        for t in range(TT):
                            last = mm(front[f"av{k}"][:, (i % 2) * D:(i % 2 + 1) * D], probT[:, t, i * P:(i + 1) * P], xn[:, t, :],
                                      start=t == 0, stop=t == TT - 1)
                    last.then_inc(front.fill_sem(f"av{k}"), 1)
                done(pe, "q_ready", b)
                front.may_fill(pe, "qT", b, done, before)
                qp = front["qT"][:, :].bitcast(bf16)
                for c in range(DC):
                    for j in range(TT):
                        last = tr(qp[:, c * T + j * P:c * T + (j + 1) * P], qb[:, j, c * P:(c + 1) * P], identb[:, :])
                last.then_inc(front.fill_sem("qT"), 1)
                done(pe, "qT_ready", b)
                for k in range(2):
                    front.may_fill(pe, f"ffn{k}", b, done, before)
                    for j in (2 * k, 2 * k + 1):
                        for c in range(DC):
                            last = mm(front[f"ffn{k}"][:, (j % 2) * D:(j % 2 + 1) * D], qT[:, c, j * P:(j + 1) * P], kq[:, c, :],
                                      start=c == 0, stop=c == DC - 1)
                    last.then_inc(front.fill_sem(f"ffn{k}"), 1)
                done(pe, "r4_ready", b)
                for c in range(DC):
                    front.may_fill(pe, f"r4T{c}", b, done, before)
                    for j in range(TT):
                        last = tr(front[f"r4T{c}"][:, j * P:(j + 1) * P], r4[:, j, c * P:(c + 1) * P], ident[:, :])
                    last.then_inc(front.fill_sem(f"r4T{c}"), 1)
                done(pe, "r4T_ready", b)
                for m in range(2 * MC):
                    front.may_fill(pe, f"in{m}", b, done, before)
                    for c in range(DC):
                        last = mm(front[f"in{m}"][:, :], w_in[:, c, m * P:(m + 1) * P], r4T[:, c, :], start=c == 0, stop=c == DC - 1)
                    last.then_inc(front.fill_sem(f"in{m}"), 1)
                done(pe, "u_ready", b)
                front.may_fill(pe, "xB", b, done, before)
                for k in range(MC):
                    last = mm(front["xB"][0:NS, :], w_x[:, k, 0:NS], u[:, k, :], start=k == 0, stop=k == MC - 1)
                last.then_inc(front.fill_sem("xB"), 1)
                front.may_fill(pe, "xC", b, done, before)
                for t in range(TT):
                    for k in range(MC):
                        last = mm(front["xC"][:, t * NS:(t + 1) * NS], u[:, k, t * P:(t + 1) * P], w_x[:, k, NS:2 * NS],
                                  start=k == 0, stop=k == MC - 1)
                last.then_inc(front.fill_sem("xC"), 1)
                for m in range(MC):
                    front.may_fill(pe, f"dt{m}", b, done, before)
                    for k in range(MC):
                        last = mm(front[f"dt{m}"][:, :], w_dt[:, k, m * P:(m + 1) * P], u[:, k, :], start=k == 0, stop=k == MC - 1)
                    last.then_inc(front.fill_sem(f"dt{m}"), 1)
                for s in range(NS):
                    done(pe, "scan_done", b, s * MC + MC - 1)
                    for t in range(TT):
                        back.may_fill(pe, f"hT{s}.{t}", b, done, before)
                        for m in range(MC):
                            last = tr(back[f"hT{s}.{t}"][:, m * P:(m + 1) * P], h[:, s % 2, m, t * P:(t + 1) * P], ident[:, :])
                        last.then_inc(back.fill_sem(f"hT{s}.{t}"), 1)
                done(pe, "acc_ready", b)
                for m in range(MC):
                    back.may_fill(pe, f"yT{m}", b, done, before)
                    for t in range(TT):
                        last = tr(back[f"yT{m}"][:, t * P:(t + 1) * P], acc[:, t, m * P:(m + 1) * P], ident[:, :])
                    last.then_inc(back.fill_sem(f"yT{m}"), 1)
                done(pe, "y3_ready", b)
                for k in range(2):
                    back.may_fill(pe, f"out{k}", b, done, before)
                    for j in (2 * k, 2 * k + 1):
                        for m in range(MC):
                            last = mm(back[f"out{k}"][:, (j % 2) * D:(j % 2 + 1) * D], y3[:, m, j * P:(j + 1) * P], w_out[:, m, :],
                                      start=m == 0, stop=m == MC - 1)
                    last.then_inc(back.fill_sem(f"out{k}"), 1)
                done(pe, "x4_ready", b)
                for c in range(DC):
                    back.may_fill(pe, f"x4T{c}", b, done, before)
                    for j in range(TT):
                        last = tr(back[f"x4T{c}"][:, j * P:(j + 1) * P], x4[:, j, c * P:(c + 1) * P], ident[:, :])
                    last.then_inc(back.fill_sem(f"x4T{c}"), 1)
                done(pe, "x4T_ready", b)
                back.may_fill(pe, "logit", b, done, before)
                for j in range(TT):
                    for c in range(DC):
                        last = mm(back["logit"][:, j * (E + 1):(j + 1) * (E + 1)], x4T[:, c, j * P:(j + 1) * P], w_gate[:, c, :],
                                  start=c == 0, stop=c == DC - 1)
                last.then_inc(back.fill_sem("logit"), 1)


def experts(nc, sem, a, out, ident, oh, topw, sharew, banks, x3_d, x4_d, xs_d, ys_d):
    ctx = ExitStack()
    with ctx:
        def sb(name, shape, dt=fp32):
            return ctx.enter_context(nc.sbuf_tensor(name, shape, dt))

        def sems(name):
            return [sem(f"{name}{k}") for k in range(2)]

        IC = [(0, 128), (128, 128), (256, 96)]
        SC = [(c * P, min(P, SI - c * P)) for c in range((SI + P - 1) // P)]

        ND = 4

        w_gu = sb("w_gu", [P, E, DC, 2 * I])
        w_dn = sb("w_dn", [P, E, len(IC), D])
        w_su = sb("w_su", [P, DC, 2 * SI])
        w_sd = sb("w_sd", [P, len(SC), D])
        tri = sb("tri", [P, P])
        ones = sb("ones", [P, NT])
        ones_p = sb("ones_p", [P, P])
        both = sb("both", [P, NT, E])
        cnt = sb("cnt", [P, NT, E])
        run = sb("run", [P, NT, E])
        padf, padi = sb("padf", [P, E]), sb("padi", [P, E], i32)
        padded, ends = sb("padded", [P, E]), sb("ends", [P, E])
        offs = sb("offs", [P, E])
        slot = sb("slot", [P, NT, E])
        prod = sb("prod", [P, NT, E])
        posf = sb("posf", [P, 2, NT])
        pos = sb("pos", [P, 2, NT], u32)
        tstart = sb("tstart", [1, SLOTS_T])
        eid, eidi = sb("eid", [1, SLOTS_T]), sb("eidi", [1, SLOTS_T], i32)
        idx = sb("idx", [P, ND, 2], u32)
        xrow = sb("xrow", [P, ND, D])

        w_loaded, w_sloaded = sem("ew_loaded"), sem("sw_loaded")
        waited = sem("waited_")
        tri_made, ones_made, tst_made, both_made = sem("tri_made"), sem("ones_made"), sem("tst_made"), sem("both_made")
        counted, chain, pos_ready = sem("counted"), sem("pos_chain"), sem("pos_ready")
        row_in = [sem(f"row_in{k}") for k in range(ND)]
        idx_copied = [sem(f"idx_copied{k}") for k in range(ND)]
        row_free = [sem(f"row_free{k}") for k in range(ND)]
        dispatched = [sem(f"dispatched{k}") for k in range(ND)]

        xe, xeT = sb("xe", [P, 2, D]), sb("xeT", [P, 2, DC, P])
        gt, gg, hh = sb("gt", [P, 2, I]), sb("gg", [P, 2, I]), sb("hh", [P, 2, I])
        hT = sb("hT", [P, 2, len(IC), P])
        ye = sb("ye", [P, 2, D])
        xe_in, xe_T, xeT_ready = sems("xe_in"), sems("xe_T"), sems("xeT_ready")
        g_full, u_full, gt_ready, gg_ready, hh_ready = sems("g_full"), sems("u_full"), sems("gt_ready"), sems("gg_ready"), sems("hh_ready")
        h_T, hT_ready, y_full, ye_ready, ye_out = sems("h_T"), sems("hT_ready"), sems("y_full"), sems("ye_ready"), sems("ye_out")

        xs, x3s, xsT = sb("xs", [P, 2, D]), sb("x3s", [P, 2, D]), sb("xsT", [P, 2, DC, P])
        sht, shg = sb("sht", [P, 2, len(SC), P]), sb("shg", [P, 2, len(SC), P])
        shh = sb("shh", [P, 2, len(SC), P])
        ids = sb("ids", [P, 2, 2], u32)
        y1s, y2s = sb("y1s", [P, 2, D]), sb("y2s", [P, 2, D])
        s1, s2, s3, fin = sb("s1", [P, 2, D]), sb("s2", [P, 2, D]), sb("s3", [P, 2, D]), sb("fin", [P, 2, D])
        rows_in, ids_ready, y1_in, y2_in = sems("rows_in"), sems("ids_ready"), sems("y1_in"), sems("y2_in")
        xs_T, xsT_ready = sems("xs_T"), sems("xsT_ready")
        sg_full, sht_ready, shg_ready, su_full, shh_ready, sd_full = (sem(n) for n in (
            "sg_full", "sht_ready", "shg_ready", "su_full", "shh_ready", "sd_full"))
        s1_ready, s2_ready, s3_ready, fin_ready, stored = (sems(n) for n in (
            "s1_ready", "s2_ready", "s3_ready", "fin_ready", "stored"))

        with nc.Block() as block:

            @block.sync
            def _(sp_):
                gu_v = a["e_gu"].rearrange("e (c p) n -> e p c n", p=P)
                for e in range(E):
                    sp_.dma_start(w_gu[:, e, :, :], gu_v[e, :, :, :]).then_inc(w_loaded, 16)
                    for k, (at, size) in enumerate(IC):
                        sp_.dma_start(w_dn[0:size, e, k, :], a["e_dn"][e, at:at + size, :]).then_inc(w_loaded, 16)
                for half, name in enumerate(("s_g", "s_u")):
                    sp_.dma_start(w_su[:, :, half * SI:(half + 1) * SI], a[name].rearrange("(c p) n -> p c n", p=P)).then_inc(w_sloaded, 16)
                for k, (at, size) in enumerate(SC):
                    sp_.dma_start(w_sd[0:size, k, :], a["s_dn"][at:at + size, :]).then_inc(w_sloaded, 16)
                for k in range(ND):
                    sp_.sem_inc(row_free[k], 1)
                with sp_.Fori(0, NT // ND) as t:
                    for k in range(ND):
                        sp_.wait_ge(row_free[k], t + 1)
                        sp_.dma_start(xrow[:, k, :], x4_d[bass.ds((t * ND + k) * P, P), :]).then_inc(row_in[k], 16)
                sp_.wait_ge(w_loaded, 16 * E * (1 + len(IC)))
                sp_.wait_ge(w_sloaded, 16 * (2 + len(SC)))

            @block.gpsimd
            def _(pool):
                g = nc.gpsimd
                g.memset(tri[:, :], 1.0).then_inc(ones_made, 1)
                g.memset(ones[:, :], 1.0).then_inc(ones_made, 1)
                g.memset(ones_p[:, :], 1.0).then_inc(ones_made, 1)
                pool.wait_ge(ones_made, 3)
                g.affine_select(out=tri[:, :], in_=tri[:, :], compare_op=ALU.is_gt, fill=0.0, base=0,
                                pattern=[[1, P]], channel_multiplier=-1).then_inc(tri_made, 1)
                g.iota(tstart[:, :], pattern=[[P, SLOTS_T]], base=0, channel_multiplier=0,
                       allow_small_or_imprecise_dtypes=True).then_inc(tst_made, 1)
                pool.wait_ge(pos_ready, 1)
                with pool.Fori(0, NT // ND) as t:
                    for k in range(ND):
                        pool.wait_ge(row_in[k], t * 16 + 16)
                        for w in range(2):
                            last = g.tensor_copy(idx[:, k, w:w + 1], pos[:, w, bass.ds(t * ND + k, 1)])
                        last.then_inc(idx_copied[k], 1)
                        pool.wait_ge(idx_copied[k], t + 1)
                        pool.sem_inc(waited, 1)
                        for w in range(2):
                            g.indirect_dma_start(xs_d, bass.IndirectOffsetOnAxis(idx[:, k, w:w + 1], 0), xrow[:, k, :], None)\
                                .then_inc(dispatched[k], 16)
                    for k in range(ND):
                        pool.wait_ge(dispatched[k], t * 32 + 32)
                        pool.sem_inc(row_free[k], 1)

            @block.tensor
            def _(pe):
                pe.wait_ge(both_made, 1)
                pe.wait_ge(tri_made, 1)
                bf = both[:, :, :].rearrange("p t e -> p (t e)")
                nc.tensor.matmul(banks[0][:, :], tri[:, :], bf, start=True, stop=True).then_inc(counted, 1)
                nc.tensor.matmul(banks[1][:, :], ones_p[:, :], bf, start=True, stop=True).then_inc(counted, 1)

            @block.vector
            def _(dve):
                v = nc.vector
                n = [0]

                def link(ins):
                    n[0] += 1
                    ins.then_inc(chain, 1)
                    dve.wait_ge(chain, n[0])

                v.tensor_tensor(both[:, :, :], oh[:, 0, :, :], oh[:, 1, :, :], ALU.add).then_inc(both_made, 1)
                dve.wait_ge(counted, 2)
                dve.wait_ge(ones_made, 3)
                link(v.tensor_copy(cnt[:, :, :], banks[1][:, :].rearrange("p (t e) -> p t e", e=E)))
                for e in range(E):
                    last = v.tensor_tensor_scan(run[:, :, e], ones[:, :], cnt[:, :, e], 0.0, ALU.mult, ALU.add)
                link(last)
                link(v.tensor_scalar(padf[:, :], run[:, NT - 1, :], float(P - 1), None, ALU.add))
                link(v.tensor_copy(padi[:, :], padf[:, :]))
                link(v.tensor_scalar(padi[:, :], padi[:, :], -P, None, ALU.bitwise_and))
                link(v.tensor_copy(padded[:, :], padi[:, :]))
                link(v.tensor_tensor_scan(ends[:, :], ones[:, 0:E], padded[:, :], 0.0, ALU.mult, ALU.add))
                link(v.tensor_tensor(offs[:, :], ends[:, :], padded[:, :], ALU.subtract))
                link(v.tensor_tensor(slot[:, :, :], run[:, :, :], cnt[:, :, :], ALU.subtract))
                link(v.tensor_tensor(slot[:, :, :], slot[:, :, :], banks[0][:, :].rearrange("p (t e) -> p t e", e=E), ALU.add))
                link(v.tensor_tensor(slot[:, :, :], slot[:, :, :], offs[:, :].unsqueeze(1).broadcast_to([P, NT, E]), ALU.add))
                for w in range(2):
                    link(v.tensor_tensor(prod[:, :, :], slot[:, :, :], oh[:, w, :, :], ALU.mult))
                    link(v.tensor_reduce(posf[:, w, :], prod[:, :, :], AX.X, ALU.add))
                v.tensor_copy(pos[:, :, :], posf[:, :, :]).then_inc(pos_ready, 1)
                dve.wait_ge(tst_made, 1)
                link(v.tensor_scalar(eid[:, :], tstart[:, :], ends[0:1, 0:1], None, ALU.is_ge))
                for e in range(1, E - 1):
                    link(v.scalar_tensor_tensor(eid[:, :], tstart[:, :], ends[0:1, e:e + 1], eid[:, :], ALU.is_ge, ALU.add))
                link(v.tensor_copy(eidi[:, :], eid[:, :]))

        freeing = (xeT_ready, gg_ready, hh_ready, hT_ready, ye_ready, xe_T, h_T, y_full, gt_ready)
        xs_v, ys_v = (d.rearrange("(g p) d -> g p d", p=P) for d in (xs_d, ys_d))
        with nc.Block() as block:
            @block.sync
            def _(sp_):
                for k in range(2):
                    for s in freeing:
                        sp_.sem_inc(s[k], 1)
                    sp_.sem_inc(ye_out[k], 16)
                with sp_.Fori(0, SLOTS_T // 2) as t:
                    for k in range(2):
                        sp_.wait_ge(xe_T[k], t + 1)
                        sp_.dma_start(xe[:, k, :], xs_d[bass.ds((t * 2 + k) * P, P), :]).then_inc(xe_in[k], 16)

            @block.tensor
            def _(pe):
                mm, tr = nc.tensor.matmul, nc.tensor.transpose
                with pe.Fori(0, SLOTS_T // 2) as t:
                    for k in range(2):
                        e = pe.value_load(eidi[0:1, bass.ds(t * 2 + k, 1)], min_val=0, max_val=E - 1)
                        pe.wait_ge(xe_in[k], t * 16 + 16)
                        pe.wait_ge(ye_ready[k], t + 1)
                        for c in range(DC):
                            last = tr(banks[4 + k][:, c * P:(c + 1) * P], xe[:, k, c * P:(c + 1) * P], ident[:, :])
                        last.then_inc(xe_T[k], 1)
                        pe.wait_ge(xeT_ready[k], t + 2)
                        pe.wait_ge(hh_ready[k], t + 1)
                        for half, full in ((0, g_full), (1, u_full)):
                            for c in range(DC):
                                last = mm(banks[2 * k + half][:, 0:I], xeT[:, k, c, :],
                                          w_gu[:, bass.ds(e, 1), c, half * I:(half + 1) * I].rearrange("p a n -> p (a n)"),
                                          start=c == 0, stop=c == DC - 1)
                            last.then_inc(full[k], 1)
                        pe.wait_ge(hh_ready[k], t + 2)
                        pe.wait_ge(hT_ready[k], t + 1)
                        for n, (at, size) in enumerate(IC):
                            last = tr(banks[6 + k][0:size, n * P:(n + 1) * P], hh[:, k, at:at + size], ident[:, :])
                        last.then_inc(h_T[k], 1)
                        pe.wait_ge(hT_ready[k], t + 2)
                        for n, (at, size) in enumerate(IC):
                            last = mm(banks[4 + k][:, 0:D], hT[0:size, k, n, :],
                                      w_dn[0:size, bass.ds(e, 1), n, :].rearrange("p a n -> p (a n)"),
                                      start=n == 0, stop=n == len(IC) - 1)
                        last.then_inc(y_full[k], 1)

            @block.scalar
            def _(act):
                f = nc.scalar.activation
                with act.Fori(0, SLOTS_T // 2) as t:
                    for k in range(2):
                        act.wait_ge(xe_T[k], t + 2)
                        f(xeT[:, k, :, :], banks[4 + k][:, 0:D].rearrange("p (c n) -> p c n", c=DC), ACT.Copy)\
                            .then_inc(xeT_ready[k], 1)
                        act.wait_ge(g_full[k], t + 1)
                        f(gt[:, k, :], banks[2 * k][:, 0:I], ACT.Tanh, scale=0.5).then_inc(gt_ready[k], 1)
                        act.wait_ge(h_T[k], t + 2)
                        f(hT[:, k, 0:2, :], banks[6 + k][:, 0:2 * P].rearrange("p (c n) -> p c n", c=2), ACT.Copy)
                        f(hT[0:IC[2][1], k, 2, :], banks[6 + k][0:IC[2][1], 2 * P:3 * P], ACT.Copy).then_inc(hT_ready[k], 1)
                        act.wait_ge(y_full[k], t + 2)
                        act.wait_ge(ye_out[k], t * 16 + 16)
                        f(ye[:, k, :], banks[4 + k][:, 0:D], ACT.Copy).then_inc(ye_ready[k], 1)
                        act.wait_ge(ye_ready[k], t + 2)
                        act.dma_start(ys_d[bass.ds((t * 2 + k) * P, P), :], ye[:, k, :]).then_inc(ye_out[k], 16)
                for k in range(2):
                    act.wait_ge(ye_out[k], 16 + 16 * (SLOTS_T // 2))

            @block.vector
            def _(dve):
                v = nc.vector
                with dve.Fori(0, SLOTS_T // 2) as t:
                    for k in range(2):
                        dve.wait_ge(gt_ready[k], t + 2)
                        v.scalar_tensor_tensor(gg[:, k, :], gt[:, k, :], 1.0, banks[2 * k][:, 0:I], ALU.add, ALU.mult)\
                            .then_inc(gg_ready[k], 1)
                        dve.wait_ge(gg_ready[k], t + 2)
                        dve.wait_ge(u_full[k], t + 1)
                        v.scalar_tensor_tensor(hh[:, k, :], gg[:, k, :], 0.5, banks[2 * k + 1][:, 0:I], ALU.mult, ALU.mult)\
                            .then_inc(hh_ready[k], 1)

        shared_freeing = (xs_T, xsT_ready, s1_ready, s2_ready, s3_ready, fin_ready, ids_ready)
        flat = out.rearrange("b t d -> (b t) d")
        with nc.Block() as block:
            @block.sync
            def _(sp_):
                for k in range(2):
                    for s in shared_freeing:
                        sp_.sem_inc(s[k], 1)
                    sp_.sem_inc(stored[k], 16)
                for s in (sht_ready, shg_ready, shh_ready):
                    sp_.sem_inc(s, 1)
                with sp_.Fori(0, NT // 2) as t:
                    for k in range(2):
                        sp_.wait_ge(xs_T[k], t + 1)
                        sp_.wait_ge(fin_ready[k], t + 1)
                        sp_.dma_start(xs[:, k, :], x4_d[bass.ds((t * 2 + k) * P, P), :]).then_inc(rows_in[k], 16)
                        sp_.dma_start(x3s[:, k, :], x3_d[bass.ds((t * 2 + k) * P, P), :]).then_inc(rows_in[k], 16)

            @block.gpsimd
            def _(pool):
                g = nc.gpsimd
                with pool.Fori(0, NT // 2) as t:
                    for k in range(2):
                        pool.wait_ge(s3_ready[k], t + 1)
                        for w in range(2):
                            last = g.tensor_copy(ids[:, k, w:w + 1], pos[:, w, bass.ds(t * 2 + k, 1)])
                        last.then_inc(ids_ready[k], 1)
                        pool.wait_ge(ids_ready[k], t + 2)
                        pool.sem_inc(waited, 1)
                        for w, (ys, s) in enumerate(((y1s, y1_in), (y2s, y2_in))):
                            g.indirect_dma_start(ys[:, k, :], None, ys_d, bass.IndirectOffsetOnAxis(ids[:, k, w:w + 1], 0))\
                                .then_inc(s[k], 16)

            @block.tensor
            def _(pe):
                mm, tr = nc.tensor.matmul, nc.tensor.transpose
                with pe.Fori(0, NT // 2) as t:
                    for k in range(2):
                        pe.wait_ge(rows_in[k], t * 32 + 32)
                        pe.wait_ge(s3_ready[k], t + 1)
                        for c in range(DC):
                            last = tr(banks[6 + k][:, c * P:(c + 1) * P], xs[:, k, c * P:(c + 1) * P], ident[:, :])
                        last.then_inc(xs_T[k], 1)
                    for k in range(2):
                        pe.wait_ge(xsT_ready[k], t + 2)
                    for half, full in ((0, sg_full), (1, su_full)):
                        for n, (at, size) in enumerate(SC):
                            if n % 2 == 0:
                                pe.wait_ge(shh_ready, t + 1)
                            for c in range(DC):
                                last = mm(banks[half * 3 + n // 2][0:size, (n % 2) * 2 * P:(n % 2 + 1) * 2 * P],
                                          w_su[:, c, half * SI + at:half * SI + at + size],
                                          xsT[:, :, c, :], start=c == 0, stop=c == DC - 1)
                        last.then_inc(full, 1)
                    pe.wait_ge(shh_ready, t + 2)
                    for k in range(2):
                        for n, (at, size) in enumerate(SC):
                            last = mm(banks[6 + k][:, 0:D], shh[0:size, k, n, :], w_sd[0:size, n, :],
                                      start=n == 0, stop=n == len(SC) - 1)
                    last.then_inc(sd_full, 1)

            def chunk(buf, n):
                return buf[0:SC[n][1], :, n, :]

            @block.scalar
            def _(act):
                f = nc.scalar.activation
                with act.Fori(0, NT // 2) as t:
                    for k in range(2):
                        act.wait_ge(xs_T[k], t + 2)
                        f(xsT[:, k, :, :], banks[6 + k][:, 0:D].rearrange("p (c n) -> p c n", c=DC), ACT.Copy)\
                            .then_inc(xsT_ready[k], 1)
                    act.wait_ge(sg_full, t + 1)
                    for n, (at, size) in enumerate(SC):
                        last = f(chunk(sht, n), banks[n // 2][0:size, (n % 2) * 2 * P:(n % 2 + 1) * 2 * P].rearrange("p (k n) -> p k n", k=2),
                                 ACT.Tanh, scale=0.5)
                    last.then_inc(sht_ready, 1)
                    for k in range(2):
                        act.wait_ge(fin_ready[k], t + 2)
                        act.dma_start(flat[bass.ds((t * 2 + k) * P, P), :], fin[:, k, :]).then_inc(stored[k], 16)
                for k in range(2):
                    act.wait_ge(stored[k], 16 + 16 * (NT // 2))

            @block.vector
            def _(dve):
                v = nc.vector
                with dve.Fori(0, NT // 2) as t:
                    dve.wait_ge(sht_ready, t + 2)
                    for n, (at, size) in enumerate(SC):
                        last = v.scalar_tensor_tensor(chunk(shg, n), chunk(sht, n), 1.0,
                                                      banks[n // 2][0:size, (n % 2) * 2 * P:(n % 2 + 1) * 2 * P].rearrange("p (k n) -> p k n", k=2),
                                                      ALU.add, ALU.mult)
                    last.then_inc(shg_ready, 1)
                    dve.wait_ge(shg_ready, t + 2)
                    dve.wait_ge(su_full, t + 1)
                    for n, (at, size) in enumerate(SC):
                        last = v.scalar_tensor_tensor(chunk(shh, n), chunk(shg, n), 0.5,
                                                      banks[3 + n // 2][0:size, (n % 2) * 2 * P:(n % 2 + 1) * 2 * P].rearrange("p (k n) -> p k n", k=2),
                                                      ALU.mult, ALU.mult)
                    last.then_inc(shh_ready, 1)
                    for k in range(2):
                        dve.wait_ge(y1_in[k], t * 16 + 16)
                        dve.wait_ge(rows_in[k], t * 32 + 32)
                        v.scalar_tensor_tensor(s1[:, k, :], y1s[:, k, :], wcol(topw, t * 2 + k, 0), x3s[:, k, :], ALU.mult, ALU.add)\
                            .then_inc(s1_ready[k], 1)
                        dve.wait_ge(s1_ready[k], t + 2)
                        dve.wait_ge(y2_in[k], t * 16 + 16)
                        v.scalar_tensor_tensor(s2[:, k, :], y2s[:, k, :], wcol(topw, t * 2 + k, 1), s1[:, k, :], ALU.mult, ALU.add)\
                            .then_inc(s2_ready[k], 1)
                    dve.wait_ge(sd_full, t + 1)
                    for k in range(2):
                        v.tensor_scalar(s3[:, k, :], banks[6 + k][:, 0:D], sharew[:, bass.ds(t * 2 + k, 1)], None, ALU.mult)\
                            .then_inc(s3_ready[k], 1)
                        dve.wait_ge(s3_ready[k], t + 2)
                        dve.wait_ge(stored[k], t * 16 + 16)
                        v.tensor_tensor(fin[:, k, :], s3[:, k, :], s2[:, k, :], ALU.add).then_inc(fin_ready[k], 1)


def wcol(topw, i, w):
    return topw[:, bass.ds(i, 1), w:w + 1].rearrange("p a b -> p (a b)")


def kernel(L0_attn_x, L0_attn_w_lhs, L0_attn_w_rhs, L0_ffn_kernel, L0_ffn_input_scale, L0_ffn_kernel_scale, L0_ffn_bias,
           L1_attn_norm_w, L1_attn_norm_b, L1_attn_in_proj_w, L1_attn_in_proj_b, L1_attn_conv_w, L1_attn_conv_b,
           L1_attn_x_proj_w, L1_attn_x_proj_b, L1_attn_dt_proj_w, L1_attn_dt_proj_b, L1_attn_A_log, L1_attn_D_param,
           L1_attn_out_proj_w, L1_attn_out_proj_b, L1_ffn_gate_w, L1_ffn_experts_gate_up, L1_ffn_experts_down,
           L1_ffn_shared_gate_w, L1_ffn_shared_up_w, L1_ffn_shared_down_w, L1_ffn_shared_expert_gate_w):
    import numpy as np
    import concourse.bacc as bacc
    from concourse.bass_utils import run_bass_kernel_spmd

    def t(w):
        return np.swapaxes(np.asarray(w), -1, -2)

    def column(vec):
        return np.asarray(vec).reshape(-1, P).T

    given = dict(
        x=L0_attn_x, w_lhs=column(L0_attn_w_lhs), w_rhs=column(L0_attn_w_rhs), kernel=L0_ffn_kernel, s_in=L0_ffn_input_scale,
        s_k=L0_ffn_kernel_scale, fbias=L0_ffn_bias, norm_w=column(L1_attn_norm_w), norm_b=column(L1_attn_norm_b),
        w_in=t(L1_attn_in_proj_w), in_b=column(L1_attn_in_proj_b), conv_w=L1_attn_conv_w, conv_b=column(L1_attn_conv_b),
        w_x=t(L1_attn_x_proj_w), x_bb=np.asarray(L1_attn_x_proj_b)[:NS].reshape(NS, 1), x_bc=np.asarray(L1_attn_x_proj_b)[NS:],
        w_dt=t(L1_attn_dt_proj_w), dt_b=column(L1_attn_dt_proj_b), a_log=L1_attn_A_log, d_param=column(L1_attn_D_param),
        w_out=t(L1_attn_out_proj_w), out_b=L1_attn_out_proj_b,
        w_gate=np.concatenate([t(L1_ffn_gate_w), t(L1_ffn_shared_expert_gate_w)], 1),
        e_gu=t(L1_ffn_experts_gate_up), e_dn=t(L1_ffn_experts_down),
        s_g=t(L1_ffn_shared_gate_w), s_u=t(L1_ffn_shared_up_w), s_dn=t(L1_ffn_shared_down_w))
    nc = bacc.Bacc("TRN2", target_bir_lowering=False, num_devices=1)
    arrays, aps = {}, {}
    for name, value in given.items():
        value = np.ascontiguousarray(value)
        arrays[f"in_{name}"] = value
        aps[name] = nc.dram_tensor(f"in_{name}", value.shape, mybir.dt.from_np(value.dtype), kind="ExternalInput").ap()
    out = nc.dram_tensor("out", (NB, T, D), fp32, kind="ExternalOutput").ap()
    build(nc, aps, out)
    r = run_bass_kernel_spmd(nc, [arrays], core_ids=[0])
    return r.results[0]["out"]
```

```python
import concourse.bass as bass
from concourse import mybir
from contextlib import ExitStack

NB, T, D = 16, 512, 256
P = 128
TT = T // P
DC = D // P
DI = 512
MC = DI // P
NS = 16
TAPS = 4
E, I, SI = 8, 352, 704
NT = NB * TT
SLOTS_T = NT * 2 + E
EPS = 1e-5
SC = [(c * P, min(P, SI - c * P)) for c in range((SI + P - 1) // P)]
UNITS = NS * MC

fp32 = mybir.dt.float32
bf16 = mybir.dt.bfloat16
i32 = mybir.dt.int32
u32 = mybir.dt.uint32
ALU = mybir.AluOpType
ACT = mybir.ActivationFunctionType
AX = mybir.AxisListType


class Banks:

    def __init__(self, tensors, full):
        self.tensors, self.full = tensors, full
        self.fills, self.last = [0] * len(full), [None] * len(full)
        self.uses = {}

    def add(self, name, bank, *readers):
        self.uses[name] = (bank, self.fills[bank], self.last[bank], readers)
        self.fills[bank] += 1
        self.last[bank] = name

    def may_fill(self, eng, name, b, done, before):
        bank, _, last, _ = self.uses[name]
        if last:
            for sem, i in self.uses[last][3]:
                done(eng, sem, b, i)
        else:
            for sem, _ in self.uses[self.last[bank]][3]:
                before(eng, sem, b)

    def filled(self, eng, name, b):
        bank, fills = self.uses[name][:2]
        eng.wait_ge(self.full[bank], b * self.fills[bank] + 2 + fills)

    def fill_sem(self, name):
        return self.full[self.uses[name][0]]

    def __getitem__(self, name):
        return self.tensors[self.uses[name][0]]


def build(nc, a, out):
    x3_d = nc.dram_tensor("x3_scratch", (NB * T, D), fp32, kind="Internal").ap()
    x4_d = nc.dram_tensor("x4_scratch", (NB * T, D), fp32, kind="Internal").ap()
    base_d = nc.dram_tensor("base_scratch", (NB * T, D), fp32, kind="Internal").ap()
    bd = nc.dram_tensor("b_scratch", (NB * NS, T), fp32, kind="Internal").ap()
    xs_d = nc.dram_tensor("slots_in", (SLOTS_T * P, D), fp32, kind="Internal").ap()
    ys_d = nc.dram_tensor("slots_out", (SLOTS_T * P, D), fp32, kind="Internal").ap()

    top = ExitStack()
    with top:
        def psb(name, shape, dt=fp32):
            return top.enter_context(nc.sbuf_tensor(name, shape, dt))

        taken = []

        def sem(name):
            taken.append(nc.alloc_semaphore(name=name))
            return taken[-1]

        ident = psb("ident", [P, P])
        identb = psb("identb", [P, P], bf16)
        oh = psb("oh", [P, 2, NT, E])
        topw = psb("topw", [P, NT, 2])
        sharew = psb("sharew", [P, NT])
        place = psb("weights", [P, DC * 2 * SI + len(SC) * D])
        w_su = place[:, 0:DC * 2 * SI].rearrange("p (c n) -> p c n", c=DC)
        w_sd = place[:, DC * 2 * SI:].rearrange("p (c n) -> p c n", c=len(SC))
        banks = [top.enter_context(nc.psum_tensor(f"bank{k}", [P, 512], fp32)) for k in range(8)]
        layers(nc, sem, a, ident, identb, oh, topw, sharew, place, w_su, w_sd, banks, x3_d, x4_d, bd, xs_d)
        nc.clear_and_free_semaphores(taken)
        nc.all_engine_barrier()
        experts(nc, sem, a, out, ident, oh, topw, sharew, w_su, w_sd, banks, x3_d, x4_d, base_d, xs_d, ys_d)


def layers(nc, sem, a, ident, identb, oh, topw, sharew, place, w_su, w_sd, banks, x3_d, x4_d, bd, xs_d):
    ctx = ExitStack()
    with ctx:
        def sb(name, shape, dt=fp32):
            return ctx.enter_context(nc.sbuf_tensor(name, shape, dt))

        w_in = place[:, 0:DC * 2 * DI].rearrange("p (c n) -> p c n", c=DC)
        w_dt = place[:, DC * 2 * DI:DC * 2 * DI + MC * DI].rearrange("p (c n) -> p c n", c=MC)
        w_x = sb("w_x", [P, MC, 2 * NS])
        w_out = sb("w_out", [P, MC, D])
        w_gate = sb("w_gate", [P, DC, E + 1])
        kern = sb("kern", [P, DC, D], bf16)
        kq = sb("kq", [P, DC, D], bf16)
        wl, wr = sb("wl", [P, DC]), sb("wr", [P, DC])
        s_in, s_k = sb("s_in", [P, 1]), sb("s_k", [P, 1])
        rs_in, rs_k, s_both = sb("rs_in", [P, 1]), sb("rs_k", [P, 1]), sb("s_both", [P, 1])
        fbias = sb("fbias", [P, D], bf16)
        nw, nb_ = sb("nw", [P, DC]), sb("nb_", [P, DC])
        in_b, in_bh = sb("in_b", [P, 2 * MC]), sb("in_bh", [P, 2 * MC])
        cw, cb = sb("cw", [P, MC, TAPS]), sb("cb", [P, MC])
        cwh, cbh = sb("cwh", [P, MC, TAPS]), sb("cbh", [P, MC])
        xb_b, xb_c = sb("xb_b", [NS, 1]), sb("xb_c", [P, NS])
        dt_b, dpar = sb("dt_b", [P, MC]), sb("dpar", [P, MC])
        alog, amat = sb("alog", [P, MC, NS]), sb("amat", [P, MC, NS])
        out_b = sb("out_b", [P, D])
        half, eps = sb("half", [P, TT]), sb("eps", [P, TT])
        iota8 = sb("iota8", [P, E])
        nought = sb("nought", [P, TT])

        x = sb("x", [P, TT, D])
        xn = sb("xn", [P, TT, D])
        st123, st5 = sb("st123", [P, TT, 6]), sb("st5", [P, TT, 6])
        mv = sb("mv", [P, 4, TT, 2])
        ve = sb("ve", [P, 4, TT])
        rstd, shift = sb("rstd", [P, 4, TT]), sb("shift", [P, 4, TT])
        r34 = sb("r34", [P, TT])
        xl, xr = sb("xl", [P, DC, T]), sb("xr", [P, DC, T])
        nmax, rsum, rinv = sb("nmax", [P, TT]), sb("rsum", [P, TT]), sb("rinv", [P, TT])
        prob = sb("prob", [P, TT, T])
        xc = sb("xc", [P, MC, TAPS - 1 + T])
        probT = xc[:, :, TAPS - 1:]
        x1 = sb("x1", [P, TT, D])
        r4T = sb("r4T", [P, DC, T])
        xb, yb = (r4T[:, k, :].bitcast(bf16).rearrange("p (t d) -> p t d", t=TT) for k in range(2))
        pf = prob[:, :, :].rearrange("p t n -> p (t n)")
        qs, qm = (pf[:, k * TT * D:(k + 1) * TT * D].rearrange("p (t d) -> p t d", t=TT) for k in range(2))
        qb = xb
        qT = sb("qT", [P, DC, T], bf16)
        x2 = sb("x2", [P, TT, D])
        res = sb("res", [P, TT, D])
        base3 = sb("base3", [P, 2, TT, D])
        r4 = xn
        zs, zt = sb("zs", [P, 2, MC, T]), prob
        cs = sb("cs", [P, MC, T])
        ch, ct = cs[:, 0:2, :], cs[:, 2:4, :]
        sp = cs
        u = sb("u", [P, 2, MC, T])
        delta, du = sb("delta", [P, 2, MC, T]), sb("du", [P, MC, T])
        bs = sb("bs", [NS, T])
        cT = sb("cT", [P, 2, TT, NS])
        bbc = sb("bbc", [P, 4, T])
        dbu = sb("dbu", [P, 4, T])
        h = sb("h", [P, 2, MC, T])
        acc = sb("acc", [P, TT, DI])
        zero = acc[:, 0, :]
        y2 = sb("y2", [P, 2, T])
        x4 = sb("x4", [P, TT, D])
        x4T = y2
        lg = sb("lg", [P, TT, E + 1])
        lmax, lsum, lrec = sb("lmax", [P, TT]), sb("lsum", [P, TT]), sb("lrec", [P, TT])
        lsub, lexp, score = sb("lsub", [P, TT, E]), sb("lexp", [P, TT, E]), sb("score", [P, TT, E])
        m8 = sb("m8", [P, TT, E])
        i8, f8 = sb("i8", [P, TT, E], u32), sb("f8", [P, TT, E])
        ohb = sb("ohb", [P, 2, TT, E])
        sg, sg1, sg2 = sb("sg", [P, TT]), sb("sg1", [P, TT]), sb("sg2", [P, TT])

        sems = {}
        SHARED = {"norm_stats": ["stats1", "stats2", "stats3"], "norm_mv": ["mv1", "mv2", "mv3"],
                  "norm_ve": ["ve1", "ve2", "ve3"], "norm_rstd": ["rstd1", "mean_rstd1", "shift1", "rstd2", "rstd3", "mean_rstd3", "shift3"],
                  "norm5_step": ["ve5", "rstd5", "mean_rstd5", "shift5"],
                  "inner_step": ["sq4", "mul4", "ve4", "rstd4"],
                  "q_step": ["q_scaled", "q_expo", "q_magic", "q_added", "q_rounded", "q_nan"],
                  "router_step": ["lg_ready", "lmax_ready", "lsub_ready", "lsum_ready", "lrec_ready", "score_ready", "max_ready",
                                  "idx_ready", "idxf_ready", "oh_ready", "sg1_ready", "sg2_ready"]}
        PLACE = {step: (group, i) for group, steps in SHARED.items() for i, step in enumerate(steps)}

        def S(name):
            name = PLACE.get(name, (name,))[0]
            if name not in sems:
                sems[name] = sem(name)
            return sems[name]

        PER = dict(x_loaded=1, stats5=1, mv5=1, xn_ready=1, xl_ready=DC, xr_ready=DC, neg_max=TT, prob_ready=TT,
                   inv_ready=1, probT_ready=TT, x1_ready=2, xb_ready=1, q_ready=1, qT_ready=1, yb_ready=2, yb2_ready=1,
                   x2_ready=1, res_ready=1, base_a=1, base_ready=1, r4_ready=1, r4T_ready=DC, xc_ready=MC, zh_ready=MC,
                   zt_ready=MC, zs_ready=MC, conv_first=MC, conv_tap=MC * (TAPS - 2), conv_ready=MC, conv_tanh=MC,
                   u_ready=MC, dt_raw=MC, dt_min=MC, dt_exp=MC, dt_ln=MC, delta_ready=MC, du_ready=MC, bs_ready=1,
                   b_stored=1, cT_ready=1, b_row0=4, b_row1=4, b_row2=4, b_row3=4, da_ready=UNITS, dbu_ready=UNITS,
                   scan_done=UNITS, acc_ready=NS * TT, y2_ready=MC, y3_ready=MC, x3_ready=2, x3_stored=1, x4_ready=1,
                   x4_stored=1, x4T_ready=DC, lexp_ready=1, sg_ready=1, routed=1,
                   **{group: len(steps) for group, steps in SHARED.items()})
        UNIT = {"x_loaded": 16, "b_stored": 16, "b_row0": 16, "b_row1": 16, "b_row2": 16, "b_row3": 16,
                "x3_stored": 16, "x4_stored": 16}

        def done(eng, name, b, i=None):
            name, i = PLACE.get(name, (name, i))
            n, k = PER[name], UNIT.get(name, 1)
            i = n - 1 if i is None else i
            eng.wait_ge(S(name), b * (n * k) + k * (2 + i))

        def before(eng, name, b, i=0):
            name = PLACE.get(name, (name,))[0]
            n, k = PER[name], UNIT.get(name, 1)
            if isinstance(b, int) and b == 0:
                i = max(i, 0)
            eng.wait_ge(S(name), b * (n * k) + k * (1 + i))

        attn = Banks(banks[2:3], [sem("attn_full")])
        proj = Banks(banks[0:2], [sem(f"proj_full{k}") for k in range(2)])
        late = Banks(banks[3:4], [sem("late_full")])
        scan = Banks(banks[4:6], [sem(f"scan_full{k}") for k in range(2)])
        order = [(f"xT{c}", ("xr_ready", c)) for c in range(DC)]
        order += [(f"score{i}", ("neg_max", i), ("prob_ready", i)) for i in range(TT)]
        order += [(f"probT{t}", ("probT_ready", t)) for t in range(TT)] + [(f"av{k}", ("x1_ready", k)) for k in range(2)]
        order += [("qT", ("qT_ready", 0))] + [(f"ffn{k}", ("yb_ready", k)) for k in range(2)]
        for name, *readers in order:
            attn.add(name, 0, *readers)
        order = [(f"r4T{c}", ("r4T_ready", c)) for c in range(DC)] + [(f"in{MC + m}", ("zt_ready", m)) for m in range(MC)]
        order += [(f"in{m}", ("xc_ready", m)) for m in range(MC)] + [("xB", ("bs_ready", 0))]
        order += [(f"dt{m}", ("dt_raw", m)) for m in range(MC)] + [("xC", ("cT_ready", 0))]
        for n, (name, *readers) in enumerate(order):
            proj.add(name, n % 2, *readers)
        order = [(f"hT{s}.{t}", ("acc_ready", s * TT + t)) for s in range(NS) for t in range(TT)]
        order += [(f"yT{m}", ("y2_ready", m)) for m in range(MC)]
        for n, (name, *readers) in enumerate(order):
            scan.add(name, n % 2, *readers)
        for name, reader in [(f"out{k}", ("x3_ready", k)) for k in range(2)] + \
                            [(f"x4T{c}", ("x4T_ready", c)) for c in range(DC)] + [("logit", ("lg_ready", 0))]:
            late.add(name, 0, reader)

        AT = dict(
            yT=(0, 0, 2, 2), y=(1, 2, 3, 3), out=(3, 6), x3=(7, 11), stats5=12, rstd5=12, x4=13, x4T_pe=(15, 18),
            x4T=(17, 19), logit=23, lg=26, lexp=27, score=29, route=32,
            stats3=0, rstd3=0, res=1, r4=2, r4T_pe=5, r4T=6, in_z=(9, 11, 12, 14), z=(11, 13, 14, 16), zs=(14, 15, 17, 18),
            base=14, in_x=(15, 17, 19, 21), xc=(17, 19, 21, 23), tap=(18, 20, 24, 26), conv=(19, 21, 25, 27), tanh=(20, 22, 26, 28),
            u=(22, 24, 28, 30), xB_pe=31, bs=35, dt_pe=(33, 37, 43, 49), raw=(38, 42, 48, 54), cut=(40, 44, 50, 55),
            sp_exp=(41, 45, 51, 56), xC_pe=54, cT=58, sp_ln=56, delta=60,
            stats1=5, rstd1=5, xn=7, xT=(10, 13), xl=(12, 15), scores=(16, 22, 26, 30), maxs=(19, 25, 29, 32),
            probs=(20, 26, 30, 33), probT_pe=(33, 35, 37, 39), probT=(35, 37, 39, 41), av=(42, 47), x1=(45, 51),
            stats2=52, rstd2=52, xb=54, q=56, q_add=57, qT_pe=60, qT=61, ffn_pe=(62, 63), ffn=(63, 64), x2=64)
        END = 1000
        LAG = MC + 1

        def spread(*steps):
            return [[g, next(g, END)] for g in steps]

        def issue(streams, n):
            for stream in streams:
                while stream[1] <= n:
                    stream[1] = next(stream[0], END)

        def turns(eng, scans, attention_of, projections_of, late_of, weights_here=lambda: None):
            issue(spread(attention_of(0, 0)), END - 1)
            weights_here()
            streams = spread(projections_of(0, 0), attention_of(1, 1))
            for n in range(UNITS + 1):
                issue(streams, n)

            def turn(b, par, late=True, projections=True, attention=True):
                scans(b, par, spread(*([late_of(b - 1, 1 - par)] if late else []),
                                     *([projections_of(b + 1, 1 - par)] if projections else []),
                                     *([attention_of(b + 2, par)] if attention else [])))

            turn(0, 0, late=False)
            with eng.Fori(0, NB // 2 - 2) as i:
                turn(i * 2 + 1, 1)
                turn(i * 2 + 2, 0)
            turn(NB - 3, 1)
            turn(NB - 2, 0, attention=False)
            turn(NB - 1, 1, projections=False, attention=False)
            issue(spread(late_of(NB - 1, 1)), END - 1)

        def db(n):
            return banks[6 + n % 2]

        w_loaded, w_sloaded, a_loaded, zero_ready, xs_zeroed = sem("w_loaded"), sem("w_sloaded"), sem("a_loaded"), sem("zero_ready"), sem("xs_zeroed")
        waited = sem("waited")
        id_zero, id_ready, iota_ready = sem("id_zero"), sem("id_ready"), sem("iota_ready")
        consts, kq_chain, amat_ready = sem("consts"), sem("kq_chain"), sem("amat_ready")

        small = [(wl, a["w_lhs"]), (wr, a["w_rhs"]), (s_in, a["s_in"].partition_broadcast(P)),
                 (s_k, a["s_k"].partition_broadcast(P)), (fbias, a["fbias"].partition_broadcast(P)), (nw, a["norm_w"]),
                 (nb_, a["norm_b"]), (in_b, a["in_b"]), (cw, a["conv_w"].rearrange("(m p) a k -> p m (a k)", p=P)),
                 (cb, a["conv_b"]), (xb_b, a["x_bb"]), (xb_c, a["x_bc"].partition_broadcast(P)),
                 (dt_b, a["dt_b"]), (dpar, a["d_param"]), (alog, a["a_log"].rearrange("(m p) s -> p m s", p=P)),
                 (out_b, a["out_b"].partition_broadcast(P)), (kern, a["kernel"].rearrange("(c p) n -> p c n", p=P))]
        large = [(w_in, a["w_in"].rearrange("(c p) n -> p c n", p=P)), (w_dt, a["w_dt"].rearrange("(c p) n -> p c n", p=P)),
                 (w_x, a["w_x"].rearrange("(c p) n -> p c n", p=P)), (w_out, a["w_out"].rearrange("(c p) n -> p c n", p=P)),
                 (w_gate, a["w_gate"].rearrange("(c p) n -> p c n", p=P))]

        def ap(t):
            return t if isinstance(t, bass.AP) else t[tuple(slice(None) for _ in t.shape)]

        def start_at_one(eng, names, bank_sems=()):
            for name in names:
                eng.sem_inc(S(name), UNIT.get(name, 1))
            for s in bank_sems:
                eng.sem_inc(s, 1)

        block = ctx.enter_context(nc.Block())

        @block.sync
        def _(sp_):
            start_at_one(sp_, list(PER), attn.full + proj.full + late.full + scan.full)
            x_v = a["x"].rearrange("b (j p) d -> p (b j) d", p=P)
            x3_v, x4_v = (d.rearrange("(g p) d -> p g d", p=P) for d in (x3_d, x4_d))

            def load(b):
                before(sp_, "x1_ready", b)
                sp_.dma_start(x[:, :, :], x_v[:, bass.ds(b * TT, TT), :]).then_inc(S("x_loaded"), 16)

            load(0)
            for t, src in small:
                sp_.dma_start(ap(t), src).then_inc(a_loaded, 16)
            for t, src in large:
                sp_.dma_start(ap(t), src).then_inc(w_loaded, 16)
            sp_.wait_ge(zero_ready, 1)
            xs_v = xs_d.rearrange("(g p) d -> p g d", p=P)
            for g in range(0, SLOTS_T, 2):
                sp_.dma_start(xs_v[:, g:g + 2, :], zero.rearrange("p (g d) -> p g d", g=2)).then_inc(xs_zeroed, 16)
            def rows(b, states):
                for s in states:
                    before(sp_, "dbu_ready", b, (s - 3) * MC)
                    sp_.dma_start(bbc[:, s % 4, :], bd[bass.ds(b * NS + s, 1), :].rearrange("a t -> (a t)").partition_broadcast(P))\
                        .then_inc(S(f"b_row{s % 4}"), 16)

            def store(b, par):
                done(sp_, "x3_ready", b)
                sp_.dma_start(x3_v[:, bass.ds(b * TT, TT), :], base3[:, par, :, :]).then_inc(S("x3_stored"), 16)
                done(sp_, "x4_ready", b)
                sp_.dma_start(x4_v[:, bass.ds(b * TT, TT), :], x4[:, :, :]).then_inc(S("x4_stored"), 16)

            def turn(b, par, with_late=True, with_load=True):
                if with_load:
                    load(b + 2)
                done(sp_, "b_stored", b)
                rows(b, range(0, 8))
                if with_late:
                    store(b - 1, 1 - par)
                rows(b, range(8, NS))

            load(1)
            turn(0, 0, with_late=False)
            with sp_.Fori(0, NB // 2 - 2) as i:
                turn(i * 2 + 1, 1)
                turn(i * 2 + 2, 0)
            turn(NB - 3, 1)
            turn(NB - 2, 0, with_load=False)
            done(sp_, "dt_raw", NB - 1)
            for half, name in enumerate(("s_g", "s_u")):
                sp_.dma_start(w_su[:, :, half * SI:(half + 1) * SI], a[name].rearrange("(c p) n -> p c n", p=P)).then_inc(w_sloaded, 16)
            for k, (at, size) in enumerate(SC):
                sp_.dma_start(w_sd[0:size, k, :], a["s_dn"][at:at + size, :]).then_inc(w_sloaded, 16)
            turn(NB - 1, 1, with_load=False)
            store(NB - 1, 1)
            sp_.wait_ge(w_sloaded, 16 * (2 + len(SC)))
            sp_.wait_ge(S("x3_stored"), 16 * (NB + 1))
            sp_.wait_ge(S("x4_stored"), 16 * (NB + 1))
            sp_.wait_ge(xs_zeroed, 16 * (SLOTS_T // 2))

        @block.gpsimd
        def _(pool):
            g = nc.gpsimd
            g.memset(zero, 0.0).then_inc(zero_ready, 1)
            g.memset(half[:, :], -0.5).then_inc(zero_ready, 1)
            g.memset(nought[:, :], 0.0).then_inc(zero_ready, 1)
            g.memset(eps[:, :], EPS).then_inc(zero_ready, 1)
            g.memset(ident[:, :], 0.0).then_inc(id_zero, 1)
            g.memset(identb[:, :], 0.0).then_inc(id_zero, 1)
            g.memset(xc[:, :, 0:TAPS - 1], 0.0).then_inc(zero_ready, 1)
            pool.wait_ge(id_zero, 2)
            for m in (ident, identb):
                g.affine_select(out=m[:, :], in_=m[:, :], compare_op=ALU.not_equal, fill=1.0, base=0,
                                pattern=[[-1, P]], channel_multiplier=1).then_inc(id_ready, 1)
            g.iota(iota8[:, :], pattern=[[1, E]], base=0, channel_multiplier=0,
                   allow_small_or_imprecise_dtypes=True).then_inc(iota_ready, 1)

            def rstd_of(b, n, mvn):
                done(pool, f"mv{n}", b)
                g.tensor_tensor(ve[:, mvn, :], mv[:, mvn, :, 1], eps[:, :], ALU.add).then_inc(S(f"ve{n}"), 1)
                done(pool, f"ve{n}", b)
                g.tensor_tensor(rstd[:, mvn, :], ve[:, mvn, :], half[:, :], ALU.pow).then_inc(S(f"rstd{n}"), 1)
                if n == 2:
                    return
                done(pool, f"rstd{n}", b)
                g.tensor_tensor(shift[:, mvn, :], mv[:, mvn, :, 0], rstd[:, mvn, :], ALU.mult).then_inc(S(f"mean_rstd{n}"), 1)
                done(pool, f"mean_rstd{n}", b)
                g.tensor_tensor(shift[:, mvn, :], nought[:, :], shift[:, mvn, :], ALU.subtract).then_inc(S(f"shift{n}"), 1)

            def attention_of(b, par):
                yield AT["rstd1"]
                rstd_of(b, 1, 0)
                yield AT["rstd2"]
                rstd_of(b, 2, 1)
                yield AT["q_add"]
                done(pool, "q_nan", b)
                g.tensor_tensor(qb[:, :, :], qm[:, :, :], qs[:, :, :], ALU.add).then_inc(S("q_ready"), 1)

            def projections_of(b, par):
                yield AT["rstd3"]
                rstd_of(b, 3, 2)
                done(pool, "rstd3", b)
                g.tensor_tensor(r34[:, :], rstd[:, 2, :], rstd[:, 2, :], ALU.mult).then_inc(S("sq4"), 1)
                done(pool, "sq4", b)
                g.tensor_tensor(r34[:, :], r34[:, :], mv[:, 2, :, 1], ALU.mult).then_inc(S("mul4"), 1)
                done(pool, "mul4", b)
                g.tensor_tensor(r34[:, :], r34[:, :], eps[:, :], ALU.add).then_inc(S("ve4"), 1)
                done(pool, "ve4", b)
                g.tensor_tensor(r34[:, :], r34[:, :], half[:, :], ALU.pow).then_inc(S("rstd4"), 1)
                yield AT["base"]
                before(pool, "x3_stored", b, -1)
                before(pool, "x4_ready", b, -1)
                done(pool, "x2_ready", b)
                for j in range(TT):
                    last = g.tensor_tensor(base3[:, par, j, :], x2[:, j, :], out_b[:, :], ALU.add)
                last.then_inc(S("base_a"), 1)
                done(pool, "base_a", b)
                done(pool, "res_ready", b)
                done(pool, "r4_ready", b)
                g.tensor_tensor(base3[:, par, :, :], base3[:, par, :, :], res[:, :, :], ALU.add).then_inc(S("base_ready"), 1)

            def late_of(b, par):
                yield AT["rstd5"]
                rstd_of(b, 5, 3)

            def scans(b, par, streams):
                for n in range(UNITS):
                    s, m = divmod(n, MC)
                    if n < MC:
                        if n == 0:
                            before(pool, "dbu_ready", b)
                        done(pool, "delta_ready", b, m)
                        g.tensor_tensor(du[:, m, :], delta[:, par, m, :], u[:, par, m, :], ALU.mult).then_inc(S("du_ready"), 1)
                        done(pool, "du_ready", b, m)
                    if m == 0:
                        done(pool, f"b_row{s % 4}", b, s // 4)
                    before(pool, "scan_done", b, n - 3)
                    g.tensor_tensor(dbu[:, n % 4, :], du[:, m, :], bbc[:, s % 4, :], ALU.mult).then_inc(S("dbu_ready"), 1)
                    issue(streams, n - 3)
                issue(streams, END - 1)

            turns(pool, scans, attention_of, projections_of, late_of)

        @block.scalar
        def _(act):
            f = nc.scalar.activation
            act.wait_ge(a_loaded, 16 * len(small))
            f(amat[:, :, :], alog[:, :, :], ACT.Exp).then_inc(consts, 1)
            def normed(b, n, mvn, src, dst, name):
                done(act, f"shift{n}", b)
                for j in range(TT):
                    last = f(dst[:, j, :], src[:, j, :], ACT.Identity, bias=shift[:, mvn, j:j + 1], scale=rstd[:, mvn, j:j + 1])
                last.then_inc(S(name), 1)

            def attention_of(b, par):
                yield AT["xn"]
                normed(b, 1, 0, x, xn, "xn_ready")
                for c in range(DC):
                    yield AT["xl"][c]
                    attn.filled(act, f"xT{c}", b)
                    f(xl[:, c, :], attn[f"xT{c}"][:, :], ACT.Copy, scale=wl[:, c:c + 1]).then_inc(S("xl_ready"), 1)
                    f(xr[:, c, :], attn[f"xT{c}"][:, :], ACT.Copy, scale=wr[:, c:c + 1]).then_inc(S("xr_ready"), 1)
                for i in range(TT):
                    yield AT["probs"][i]
                    done(act, "neg_max", b, i)
                    f(prob[:, i, :], attn[f"score{i}"][:, :], ACT.Exp, bias=nmax[:, i:i + 1],
                      accum_out=rsum[:, i:i + 1]).then_inc(S("prob_ready"), 1)
                for t in range(TT):
                    yield AT["probT"][t]
                    attn.filled(act, f"probT{t}", b)
                    f(probT[:, t, :], attn[f"probT{t}"][:, :], ACT.Copy).then_inc(S("probT_ready"), 1)
                yield AT["qT"]
                attn.filled(act, "qT", b)
                qp = attn["qT"][:, :].bitcast(bf16)
                f(qT[:, :, :], qp.rearrange("p (c t) -> p c t", c=DC), ACT.Copy).then_inc(S("qT_ready"), 1)
                for k in range(2):
                    yield AT["ffn"][k]
                    attn.filled(act, f"ffn{k}", b)
                    f(yb[:, 2 * k:2 * k + 2, :], attn[f"ffn{k}"][:, :].rearrange("p (j d) -> p j d", j=2), ACT.Copy,
                      scale=s_both[:, 0:1]).then_inc(S("yb_ready"), 1)

            def projections_of(b, par):
                yield AT["res"]
                normed(b, 3, 2, x2, res, "res_ready")
                yield AT["r4"]
                done(act, "res_ready", b)
                done(act, "rstd4", b)
                for j in range(TT):
                    last = f(r4[:, j, :], res[:, j, :], ACT.Copy, scale=r34[:, j:j + 1])
                last.then_inc(S("r4_ready"), 1)
                yield AT["r4T"]
                for c in range(DC):
                    proj.filled(act, f"r4T{c}", b)
                    f(r4T[:, c, :], proj[f"r4T{c}"][:, :], ACT.Identity, bias=nb_[:, c:c + 1],
                      scale=nw[:, c:c + 1]).then_inc(S("r4T_ready"), 1)

                def xc_of(m):
                    proj.filled(act, f"in{m}", b)
                    f(xc[:, m, TAPS - 1:], proj[f"in{m}"][:, :], ACT.Identity, bias=in_b[:, m:m + 1]).then_inc(S("xc_ready"), 1)

                def z_of(m):
                    proj.filled(act, f"in{MC + m}", b)
                    f(zs[:, par, m, :], proj[f"in{MC + m}"][:, :], ACT.Identity, bias=in_bh[:, MC + m:MC + m + 1], scale=0.5)\
                        .then_inc(S("zh_ready"), 1)
                    f(zt[:, m, :], proj[f"in{MC + m}"][:, :], ACT.Tanh, bias=in_bh[:, MC + m:MC + m + 1], scale=0.5)\
                        .then_inc(S("zt_ready"), 1)

                def tanh_of(m):
                    done(act, "conv_ready", b, m)
                    f(ct[:, m % 2, :], ch[:, m % 2, :], ACT.Tanh).then_inc(S("conv_tanh"), 1)

                def tap_of(m):
                    done(act, "xc_ready", b, m)
                    if m >= 2:
                        done(act, "u_ready", b, m - 2)
                    else:
                        before(act, "delta_ready", b)
                    f(ch[:, m % 2, :], xc[:, m, 0:T], ACT.Identity, bias=cbh[:, m:m + 1], scale=cwh[:, m, 0:1])\
                        .then_inc(S("conv_first"), 1)

                steps = [(AT["xc"][m], 0, xc_of, m) for m in range(MC)] + [(AT["z"][m], 1, z_of, m) for m in range(MC)] + \
                        [(AT["tap"][m], 3, tap_of, m) for m in range(MC)] + [(AT["tanh"][m], 2, tanh_of, m) for m in range(MC)]
                for at, _, step, m in sorted(steps, key=lambda x: x[:2]):
                    yield at
                    step(m)
                yield AT["bs"]
                proj.filled(act, "xB", b)
                before(act, "b_stored", b)
                f(bs[:, :], proj["xB"][0:NS, :], ACT.Identity, bias=xb_b[:, 0:1]).then_inc(S("bs_ready"), 1)
                done(act, "bs_ready", b)
                act.dma_start(bd[bass.ds(b * NS, NS), :], bs[:, :]).then_inc(S("b_stored"), 16)

                def raw_of(m):
                    proj.filled(act, f"dt{m}", b)
                    f(delta[:, par, m, :], proj[f"dt{m}"][:, :], ACT.Identity, bias=dt_b[:, m:m + 1]).then_inc(S("dt_raw"), 1)

                def exp_of(m):
                    done(act, "dt_min", b, m)
                    f(sp[:, m, :], sp[:, m, :], ACT.Exp).then_inc(S("dt_exp"), 1)

                steps = [(AT["raw"][m], 1, raw_of, m) for m in range(MC)] + [(AT["sp_exp"][m], 0 if m < MC - 1 else 2, exp_of, m) for m in range(MC)]
                for at, _, step, m in sorted(steps, key=lambda x: x[:2]):
                    yield at
                    step(m)
                yield AT["sp_ln"]
                done(act, "dt_exp", b)
                for m in range(MC):
                    f(sp[:, m, :], sp[:, m, :], ACT.Ln, bias=1.0).then_inc(S("dt_ln"), 1)

            def late_of(b, par):
                yield AT["x4"]
                before(act, "x4_stored", b)
                normed(b, 5, 3, base3[:, par], x4, "x4_ready")
                for c in range(DC):
                    yield AT["x4T"][c]
                    late.filled(act, f"x4T{c}", b)
                    f(x4T[:, c, :], late[f"x4T{c}"][:, :], ACT.Copy).then_inc(S("x4T_ready"), 1)
                yield AT["lexp"]
                done(act, "lsub_ready", b)
                f(lexp[:, :, :], lsub[:, :, :], ACT.Exp).then_inc(S("lexp_ready"), 1)
                f(sg[:, :], lg[:, :, E], ACT.Exp, scale=-1.0).then_inc(S("sg_ready"), 1)

            def scans(b, par, streams):
                for n in range(UNITS):
                    s, m = divmod(n, MC)
                    if n < MC:
                        done(act, "delta_ready", b, m)
                    before(act, "scan_done", b, n - 1)
                    f(db(n)[:, :], delta[:, par, m, :], ACT.Exp, scale=amat[:, m, s:s + 1]).then_inc(S("da_ready"), 1)
                    issue(streams, n - 1)
                issue(streams, END - 1)

            turns(act, scans, attention_of, projections_of, late_of)

        @block.vector
        def _(dve):
            v = nc.vector
            dve.wait_ge(a_loaded, 16 * len(small))
            dve.wait_ge(consts, 1)
            v.tensor_scalar(amat[:, :, :], amat[:, :, :], -1.0, None, ALU.mult).then_inc(amat_ready, 1)
            v.tensor_scalar(in_bh[:, :], in_b[:, :], 0.5, None, ALU.mult).then_inc(amat_ready, 1)
            v.tensor_scalar(cwh[:, :, :], cw[:, :, :], 0.5, None, ALU.mult)
            v.tensor_scalar(cbh[:, :], cb[:, :], 0.5, None, ALU.mult)
            v.tensor_tensor(s_both[:, :], s_in[:, :], s_k[:, :], ALU.mult)
            v.reciprocal(rs_in[:, :], s_in[:, :])
            v.reciprocal(rs_k[:, :], s_k[:, :]).then_inc(amat_ready, 1)
            dve.wait_ge(amat_ready, 3)

            def to_e4m3(x_in, scale, q, m, wait, e_sem):
                v.tensor_scalar(q, x_in, scale, None, ALU.mult).then_inc(e_sem[0], 1)
                wait(0)
                v.tensor_scalar(m.bitcast(i32), q.bitcast(i32), 0x7F800000, None, ALU.bitwise_and).then_inc(e_sem[1], 1)
                wait(1)
                v.tensor_scalar(m, m, 2.0 ** -6, 1.5 * 2.0 ** 20, ALU.max, ALU.mult).then_inc(e_sem[2], 1)
                wait(2)
                v.tensor_tensor(q, q, m, ALU.add).then_inc(e_sem[3], 1)
                wait(3)
                v.tensor_tensor(m, q, m, ALU.subtract).then_inc(e_sem[4], 1)
                wait(4)
                v.tensor_scalar(q, m, 3.4e38 / 460.0, 0.0, ALU.mult, ALU.mult).then_inc(e_sem[5], 1)

            kq_q, kq_m = qs[:, 0:DC, :], qm[:, 0:DC, :]
            to_e4m3(kern[:, :, :], rs_k[:, 0:1], kq_q, kq_m, lambda n: dve.wait_ge(kq_chain, n + 1), [kq_chain] * 6)
            dve.wait_ge(kq_chain, 6)
            v.tensor_tensor(kq[:, :, :], kq_m, kq_q, ALU.add).then_inc(kq_chain, 1)
            dve.wait_ge(kq_chain, 7)
            dve.wait_ge(zero_ready, 5)
            dve.wait_ge(iota_ready, 1)

            def stats(b, n, mvn, src):
                st = st5 if n == 5 else st123
                if n == 1:
                    before(dve, "mv1", b)
                if n == 5:
                    before(dve, "mv5", b)
                for j in range(TT):
                    last = v.bn_stats(st[:, j, :], src[:, j, :])
                last.then_inc(S(f"stats{n}"), 1)
                done(dve, f"stats{n}", b)
                dve.sem_inc(waited, 1)
                for j in range(TT):
                    last = v.bn_aggr(mv[:, mvn, j, :], st[:, j, :])
                last.then_inc(S(f"mv{n}"), 1)

            def normed(b, n, mvn, src, dst, name):
                done(dve, f"rstd{n}", b)
                for j in range(TT):
                    last = v.tensor_scalar(dst[:, j, :], src[:, j, :], mv[:, mvn, j, 0:1], rstd[:, mvn, j:j + 1],
                                           ALU.subtract, ALU.mult)
                last.then_inc(S(name), 1)

            def attention_of(b, par):
                yield AT["stats1"]
                done(dve, "x_loaded", b)
                stats(b, 1, 0, x)
                for i in range(TT):
                    yield AT["maxs"][i]
                    attn.filled(dve, f"score{i}", b)
                    v.tensor_reduce(nmax[:, i:i + 1], attn[f"score{i}"][:, :], AX.X, ALU.max, negate=True).then_inc(S("neg_max"), 1)
                for k in range(2):
                    yield AT["x1"][k]
                    if k == 0:
                        done(dve, "prob_ready", b)
                        v.reciprocal(rinv[:, :], rsum[:, :]).then_inc(S("inv_ready"), 1)
                        done(dve, "inv_ready", b)
                    attn.filled(dve, f"av{k}", b)
                    for i in (2 * k, 2 * k + 1):
                        last = v.scalar_tensor_tensor(x1[:, i, :], attn[f"av{k}"][:, (i % 2) * D:(i % 2 + 1) * D], rinv[:, i:i + 1],
                                                      x[:, i, :], ALU.mult, ALU.add)
                    last.then_inc(S("x1_ready"), 1)
                yield AT["stats2"]
                done(dve, "x1_ready", b)
                stats(b, 2, 1, x1)
                yield AT["xb"]
                normed(b, 2, 1, x1, xb, "xb_ready")
                yield AT["q"]
                done(dve, "xb_ready", b)
                names = SHARED["q_step"]
                to_e4m3(xb[:, :, :], rs_in[:, 0:1], qs[:, :, :], qm[:, :, :], lambda n: done(dve, names[n], b), [S(n) for n in names])
                yield AT["x2"]
                done(dve, "yb_ready", b)
                for j in range(TT):
                    last = v.tensor_tensor(yb[:, j, :], yb[:, j, :], fbias[:, :], ALU.add)
                last.then_inc(S("yb2_ready"), 1)
                done(dve, "yb2_ready", b)
                v.tensor_tensor(x2[:, :, :], x1[:, :, :], yb[:, :, :], ALU.add).then_inc(S("x2_ready"), 1)

            def projections_of(b, par):
                yield AT["stats3"]
                done(dve, "x2_ready", b)
                stats(b, 3, 2, x2)

                def conv(m):
                    done(dve, "conv_first", b, m)
                    for k in range(1, TAPS):
                        if k > 1:
                            done(dve, "conv_tap", b, (TAPS - 2) * m + k - 2)
                        v.scalar_tensor_tensor(ch[:, m % 2, :], xc[:, m, k:k + T], cwh[:, m, k:k + 1], ch[:, m % 2, :],
                                               ALU.mult, ALU.add).then_inc(S("conv_tap" if k < TAPS - 1 else "conv_ready"), 1)

                def u_of(m):
                    done(dve, "conv_tanh", b, m)
                    v.scalar_tensor_tensor(u[:, par, m, :], ct[:, m % 2, :], 1.0, ch[:, m % 2, :], ALU.add, ALU.mult).then_inc(S("u_ready"), 1)

                def zs_of(m):
                    done(dve, "zt_ready", b, m)
                    v.scalar_tensor_tensor(zs[:, par, m, :], zt[:, m, :], 1.0, zs[:, par, m, :], ALU.add, ALU.mult).then_inc(S("zs_ready"), 1)

                steps = [(AT["conv"][m], 1, conv, m) for m in range(MC)] + [(AT["u"][m], 0, u_of, m) for m in range(MC)] + \
                        [(AT["zs"][m], 2, zs_of, m) for m in range(MC)]
                for at, _, step, m in sorted(steps, key=lambda x: x[:2]):
                    yield at
                    step(m)
                def cut(m):
                    done(dve, "dt_raw", b, m)
                    v.tensor_scalar(sp[:, m, :], delta[:, par, m, :], 40.0, None, ALU.min).then_inc(S("dt_min"), 1)

                steps = [(AT["cut"][m], 0, cut, m) for m in range(MC)]
                for at, _, step, m in sorted(steps, key=lambda x: x[:2]):
                    yield at
                    step(m)
                yield AT["cT"]
                proj.filled(dve, "xC", b)
                v.tensor_tensor(cT[:, par, :, :], proj["xC"][:, 0:TT * NS].rearrange("p (t s) -> p t s", s=NS),
                                xb_c[:, :].unsqueeze(1).broadcast_to([P, TT, NS]), ALU.add).then_inc(S("cT_ready"), 1)
                yield AT["delta"]
                for m in range(MC):
                    done(dve, "dt_ln", b, m)
                    v.tensor_tensor(delta[:, par, m, :], delta[:, par, m, :], sp[:, m, :], ALU.max).then_inc(S("delta_ready"), 1)

            def late_of(b, par):
                for m in range(MC):
                    yield AT["y"][m]
                    scan.filled(dve, f"yT{m}", b)
                    if m >= 2:
                        done(dve, "y3_ready", b, m - 2)
                    v.scalar_tensor_tensor(y2[:, m % 2, :], u[:, par, m, :], dpar[:, m:m + 1], scan[f"yT{m}"][:, :], ALU.mult, ALU.add)\
                        .then_inc(S("y2_ready"), 1)
                    done(dve, "y2_ready", b, m)
                    v.tensor_tensor(zs[:, par, m, :], y2[:, m % 2, :], zs[:, par, m, :], ALU.mult).then_inc(S("y3_ready"), 1)
                for k in range(2):
                    yield AT["x3"][k]
                    late.filled(dve, f"out{k}", b)
                    if k == 0:
                        done(dve, "base_ready", b)
                    x3 = base3[:, par, 2 * k:2 * k + 2, :]
                    v.tensor_tensor(x3, late[f"out{k}"][:, :].rearrange("p (j d) -> p j d", j=2), x3, ALU.add).then_inc(S("x3_ready"), 1)
                yield AT["stats5"]
                done(dve, "x3_ready", b)
                stats(b, 5, 3, base3[:, par])
                yield AT["lg"]
                late.filled(dve, "logit", b)
                v.tensor_copy(lg[:, :, :], late["logit"][:, 0:TT * (E + 1)].rearrange("p (t e) -> p t e", e=E + 1)).then_inc(S("lg_ready"), 1)
                done(dve, "lg_ready", b)
                v.tensor_reduce(lmax[:, :], lg[:, :, 0:E], AX.X, ALU.max).then_inc(S("lmax_ready"), 1)
                done(dve, "lmax_ready", b)
                v.tensor_tensor(lsub[:, :, :], lg[:, :, 0:E], lmax[:, :].unsqueeze(2).broadcast_to([P, TT, E]), ALU.subtract)\
                    .then_inc(S("lsub_ready"), 1)
                yield AT["score"]
                done(dve, "lexp_ready", b)
                v.tensor_reduce(lsum[:, :], lexp[:, :, :], AX.X, ALU.add).then_inc(S("lsum_ready"), 1)
                done(dve, "lsum_ready", b)
                v.reciprocal(lrec[:, :], lsum[:, :]).then_inc(S("lrec_ready"), 1)
                done(dve, "lrec_ready", b)
                v.tensor_tensor(score[:, :, :], lexp[:, :, :], lrec[:, :].unsqueeze(2).broadcast_to([P, TT, E]), ALU.mult)\
                    .then_inc(S("score_ready"), 1)
                yield AT["route"]
                done(dve, "score_ready", b)
                dve.sem_inc(waited, 1)
                for j in range(TT):
                    last = v.max(m8[:, j, :], score[:, j, :])
                last.then_inc(S("max_ready"), 1)
                done(dve, "max_ready", b)
                dve.sem_inc(waited, 1)
                for j in range(TT):
                    last = v.max_index(i8[:, j, :], m8[:, j, :], score[:, j, :])
                last.then_inc(S("idx_ready"), 1)
                done(dve, "idx_ready", b)
                v.tensor_copy(f8[:, :, :], i8[:, :, :]).then_inc(S("idxf_ready"), 1)
                done(dve, "idxf_ready", b)
                for k in range(2):
                    for j in range(TT):
                        last = v.tensor_scalar(ohb[:, k, j, :], iota8[:, :], f8[:, j, k:k + 1], None, ALU.is_equal)
                last.then_inc(S("oh_ready"), 1)
                done(dve, "oh_ready", b)
                for k in range(2):
                    v.tensor_copy(oh[:, k, bass.ds(b * TT, TT), :], ohb[:, k, :, :])
                v.tensor_copy(topw[:, bass.ds(b * TT, TT), :], m8[:, :, 0:2])
                done(dve, "sg_ready", b)
                v.tensor_scalar(sg1[:, :], sg[:, :], 1.0, None, ALU.add).then_inc(S("sg1_ready"), 1)
                done(dve, "sg1_ready", b)
                v.reciprocal(sg2[:, :], sg1[:, :]).then_inc(S("sg2_ready"), 1)
                done(dve, "sg2_ready", b)
                v.tensor_copy(sharew[:, bass.ds(b * TT, TT)], sg2[:, :]).then_inc(S("routed"), 1)

            def scans(b, par, streams):
                def add_state(s, t):
                    scan.filled(dve, f"hT{s}.{t}", b)
                    hT, c = scan[f"hT{s}.{t}"], cT[:, par, t, s:s + 1]
                    if s == 0:
                        v.tensor_scalar(acc[:, t, :], hT[:, :], c, None, ALU.mult).then_inc(S("acc_ready"), 1)
                    else:
                        done(dve, "acc_ready", b, (s - 1) * TT + t)
                        v.scalar_tensor_tensor(acc[:, t, :], hT[:, :], c, acc[:, t, :], ALU.mult, ALU.add).then_inc(S("acc_ready"), 1)

                done(dve, "cT_ready", b)
                for n in range(UNITS):
                    s, m = divmod(n, MC)
                    issue(streams, n)
                    done(dve, "da_ready", b, n)
                    done(dve, "dbu_ready", b, n)
                    if m == 0 and s >= 2:
                        scan.filled(dve, f"hT{s - 2}.{TT - 1}", b)
                    v.tensor_tensor_scan(h[:, s % 2, m, :], db(n)[:, :], dbu[:, n % 4, :], 0.0, ALU.mult, ALU.add)\
                        .then_inc(S("scan_done"), 1)
                    if n >= LAG:
                        add_state(*divmod(n - LAG, TT))
                for k in range(UNITS - LAG, UNITS):
                    add_state(*divmod(k, TT))
                issue(streams, END - 1)

            turns(dve, scans, attention_of, projections_of, late_of, lambda: dve.wait_ge(xs_zeroed, 16 * (SLOTS_T // 2)))

        @block.tensor
        def _(pe):
            mm, tr = nc.tensor.matmul, nc.tensor.transpose
            pe.wait_ge(id_ready, 2)
            def attention_of(b, par):
                for c in range(DC):
                    yield AT["xT"][c]
                    done(pe, "xn_ready", b)
                    attn.may_fill(pe, f"xT{c}", b, done, before)
                    for j in range(TT):
                        last = tr(attn[f"xT{c}"][:, j * P:(j + 1) * P], xn[:, j, c * P:(c + 1) * P], ident[:, :])
                    last.then_inc(attn.fill_sem(f"xT{c}"), 1)
                for i in range(TT):
                    yield AT["scores"][i]
                    if i == 0:
                        done(pe, "xl_ready", b)
                        done(pe, "xr_ready", b)
                    attn.may_fill(pe, f"score{i}", b, done, before)
                    for c in range(DC):
                        last = mm(attn[f"score{i}"][:, :], xl[:, c, i * P:(i + 1) * P], xr[:, c, :], start=c == 0, stop=c == DC - 1)
                    last.then_inc(attn.fill_sem(f"score{i}"), 1)
                for t in range(TT):
                    yield AT["probT_pe"][t]
                    if t == 0:
                        done(pe, "prob_ready", b)
                    attn.may_fill(pe, f"probT{t}", b, done, before)
                    for i in range(TT):
                        last = tr(attn[f"probT{t}"][:, i * P:(i + 1) * P], prob[:, i, t * P:(t + 1) * P], ident[:, :])
                    last.then_inc(attn.fill_sem(f"probT{t}"), 1)
                for k in range(2):
                    yield AT["av"][k]
                    if k == 0:
                        done(pe, "probT_ready", b)
                    attn.may_fill(pe, f"av{k}", b, done, before)
                    for i in (2 * k, 2 * k + 1):
                        if i % 2:
                            yield AT["av"][k] + 1
                        for t in range(TT):
                            last = mm(attn[f"av{k}"][:, (i % 2) * D:(i % 2 + 1) * D], probT[:, t, i * P:(i + 1) * P], xn[:, t, :],
                                      start=t == 0, stop=t == TT - 1)
                    last.then_inc(attn.fill_sem(f"av{k}"), 1)
                yield AT["qT_pe"]
                done(pe, "q_ready", b)
                attn.may_fill(pe, "qT", b, done, before)
                qp = attn["qT"][:, :].bitcast(bf16)
                for c in range(DC):
                    for j in range(TT):
                        last = tr(qp[:, c * T + j * P:c * T + (j + 1) * P], qb[:, j, c * P:(c + 1) * P], identb[:, :])
                last.then_inc(attn.fill_sem("qT"), 1)
                if isinstance(b, int) and b == 0:
                    pe.wait_ge(kq_chain, 7)
                for k in range(2):
                    yield AT["ffn_pe"][k]
                    done(pe, "qT_ready", b)
                    attn.may_fill(pe, f"ffn{k}", b, done, before)
                    for j in (2 * k, 2 * k + 1):
                        for c in range(DC):
                            last = mm(attn[f"ffn{k}"][:, (j % 2) * D:(j % 2 + 1) * D], qT[:, c, j * P:(j + 1) * P], kq[:, c, :],
                                      start=c == 0, stop=c == DC - 1)
                    last.then_inc(attn.fill_sem(f"ffn{k}"), 1)

            def projections_of(b, par):
                yield AT["r4T_pe"]
                done(pe, "r4_ready", b)
                for c in range(DC):
                    proj.may_fill(pe, f"r4T{c}", b, done, before)
                    for j in range(TT):
                        last = tr(proj[f"r4T{c}"][:, j * P:(j + 1) * P], r4[:, j, c * P:(c + 1) * P], ident[:, :])
                    last.then_inc(proj.fill_sem(f"r4T{c}"), 1)
                for m, at in [(MC + m, AT["in_z"][m]) for m in range(MC)] + [(m, AT["in_x"][m]) for m in range(MC)]:
                    yield at
                    if m == MC:
                        done(pe, "r4T_ready", b)
                    proj.may_fill(pe, f"in{m}", b, done, before)
                    for c in range(DC):
                        if c:
                            yield at + 0.5
                        last = mm(proj[f"in{m}"][:, :], w_in[:, c, m * P:(m + 1) * P], r4T[:, c, :], start=c == 0, stop=c == DC - 1)
                    last.then_inc(proj.fill_sem(f"in{m}"), 1)
                yield AT["xB_pe"]
                done(pe, "u_ready", b)
                proj.may_fill(pe, "xB", b, done, before)
                for k in range(MC):
                    if k == 2:
                        yield AT["xB_pe"] + 1
                    last = mm(proj["xB"][0:NS, :], w_x[:, k, 0:NS], u[:, par, k, :], start=k == 0, stop=k == MC - 1)
                last.then_inc(proj.fill_sem("xB"), 1)
                for m in range(MC):
                    yield AT["dt_pe"][m]
                    proj.may_fill(pe, f"dt{m}", b, done, before)
                    for k in range(MC):
                        if k:
                            yield AT["dt_pe"][m] + k
                        last = mm(proj[f"dt{m}"][:, :], w_dt[:, k, m * P:(m + 1) * P], u[:, par, k, :], start=k == 0, stop=k == MC - 1)
                    last.then_inc(proj.fill_sem(f"dt{m}"), 1)
                yield AT["xC_pe"]
                proj.may_fill(pe, "xC", b, done, before)
                for t in range(TT):
                    for k in range(MC):
                        last = mm(proj["xC"][:, t * NS:(t + 1) * NS], u[:, par, k, t * P:(t + 1) * P], w_x[:, k, NS:2 * NS],
                                  start=k == 0, stop=k == MC - 1)
                last.then_inc(proj.fill_sem("xC"), 1)

            def late_of(b, par):
                for m in range(MC):
                    yield AT["yT"][m]
                    if m == 0:
                        done(pe, "acc_ready", b)
                    scan.may_fill(pe, f"yT{m}", b, done, before)
                    for t in range(TT):
                        last = tr(scan[f"yT{m}"][:, t * P:(t + 1) * P], acc[:, t, m * P:(m + 1) * P], ident[:, :])
                    last.then_inc(scan.fill_sem(f"yT{m}"), 1)
                for k in range(2):
                    yield AT["out"][k]
                    if k == 0:
                        done(pe, "y3_ready", b)
                    late.may_fill(pe, f"out{k}", b, done, before)
                    for j in (2 * k, 2 * k + 1):
                        if j % 2:
                            yield AT["out"][k] + 1
                        for m in range(MC):
                            last = mm(late[f"out{k}"][:, (j % 2) * D:(j % 2 + 1) * D], zs[:, par, m, j * P:(j + 1) * P], w_out[:, m, :],
                                      start=m == 0, stop=m == MC - 1)
                    last.then_inc(late.fill_sem(f"out{k}"), 1)
                for c in range(DC):
                    yield AT["x4T_pe"][c]
                    if c == 0:
                        done(pe, "x4_ready", b)
                    late.may_fill(pe, f"x4T{c}", b, done, before)
                    for j in range(TT):
                        last = tr(late[f"x4T{c}"][:, j * P:(j + 1) * P], x4[:, j, c * P:(c + 1) * P], ident[:, :])
                    last.then_inc(late.fill_sem(f"x4T{c}"), 1)
                yield AT["logit"]
                done(pe, "x4T_ready", b)
                late.may_fill(pe, "logit", b, done, before)
                for j in range(TT):
                    for c in range(DC):
                        last = mm(late["logit"][:, j * (E + 1):(j + 1) * (E + 1)], x4T[:, c, j * P:(j + 1) * P], w_gate[:, c, :],
                                  start=c == 0, stop=c == DC - 1)
                last.then_inc(late.fill_sem("logit"), 1)

            def scans(b, par, streams):
                def transpose_state(s, t):
                    if t == 0:
                        done(pe, "scan_done", b, s * MC + MC - 1)
                    scan.may_fill(pe, f"hT{s}.{t}", b, done, before)
                    for m in range(MC):
                        last = tr(scan[f"hT{s}.{t}"][:, m * P:(m + 1) * P], h[:, s % 2, m, t * P:(t + 1) * P], ident[:, :])
                    last.then_inc(scan.fill_sem(f"hT{s}.{t}"), 1)

                for n in range(UNITS):
                    s, m = divmod(n, MC)
                    if s > 0:
                        for t in ((0, 1), (), (2,), (3,))[m]:
                            transpose_state(s - 1, t)
                    issue(streams, n)
                for t in range(TT):
                    transpose_state(NS - 1, t)
                issue(streams, END - 1)

            turns(pe, scans, attention_of, projections_of, late_of, lambda: pe.wait_ge(w_loaded, 16 * len(large)))


def experts(nc, sem, a, out, ident, oh, topw, sharew, w_su, w_sd, banks, x3_d, x4_d, base_d, xs_d, ys_d):
    ctx = ExitStack()
    with ctx:
        def sb(name, shape, dt=fp32):
            return ctx.enter_context(nc.sbuf_tensor(name, shape, dt))

        def sems(name):
            return [sem(f"{name}{k}") for k in range(2)]

        IC = [(0, 128), (128, 128), (256, 96)]

        ND = 4

        w_gu = sb("w_gu", [P, E, DC, 2 * I])
        w_dn = sb("w_dn", [P, E, len(IC), D])
        tri = sb("tri", [P, P])
        ones = sb("ones", [P, NT])
        ones_p = sb("ones_p", [P, P])
        both = sb("both", [P, NT, E])
        cnt = sb("cnt", [P, NT, E])
        run = sb("run", [P, NT, E])
        padf, padi = sb("padf", [P, E]), sb("padi", [P, E], i32)
        padded, ends = sb("padded", [P, E]), sb("ends", [P, E])
        offs = sb("offs", [P, E])
        slot = sb("slot", [P, NT, E])
        prod = sb("prod", [P, NT, E])
        posf = sb("posf", [P, 2, NT])
        pos = sb("pos", [P, 2, NT], u32)
        tstart = sb("tstart", [1, SLOTS_T])
        eid, eidi = sb("eid", [1, SLOTS_T]), sb("eidi", [1, SLOTS_T], i32)
        idx = sb("idx", [P, ND, 2], u32)
        xrow = sb("xrow", [P, ND, D])

        w_loaded = sem("ew_loaded")
        waited = sem("waited_")
        tri_made, ones_made, tst_made, both_made = sem("tri_made"), sem("ones_made"), sem("tst_made"), sem("both_made")
        counted, chain, pos_ready = sem("counted"), sem("pos_chain"), sem("pos_ready")
        row_in = [sem(f"row_in{k}") for k in range(ND)]
        idx_copied = [sem(f"idx_copied{k}") for k in range(ND)]
        row_free = [sem(f"row_free{k}") for k in range(ND)]
        dispatched = [sem(f"dispatched{k}") for k in range(ND)]

        xe, xeT = sb("xe", [P, 2, D]), sb("xeT", [P, 2, DC, P])
        gt, gg, hh = sb("gt", [P, 2, I]), sb("gg", [P, 2, I]), sb("hh", [P, 2, I])
        hT = sb("hT", [P, 2, len(IC), P])
        ye = sb("ye", [P, 2, D])
        xe_in, xe_T, xeT_ready = sems("xe_in"), sems("xe_T"), sems("xeT_ready")
        g_full, u_full, gt_ready, gg_ready, hh_ready = sems("g_full"), sems("u_full"), sems("gt_ready"), sems("gg_ready"), sems("hh_ready")
        h_T, hT_ready, y_full, ye_ready, ye_out = sems("h_T"), sems("hT_ready"), sems("y_full"), sems("ye_ready"), sems("ye_out")

        xs, x3s, xsT = sb("xs", [P, 2, D]), sb("x3s", [P, 2, 2, D]), sb("xsT", [P, 2, 2, DC, P])
        sht, shg = sb("sht", [P, len(SC), 2, P]), sb("shg", [P, len(SC), 2, P])
        shh = sb("shh", [P, 2, len(SC), 2, P])
        sbase = sb("sbase", [P, 2, D])
        xs_in, x3s_in = sems("xs_in"), sems("x3s_in")
        xs_T, xsT_ready, sg_full, sht_ready, shg_ready, su_full, shh_ready, sd_full, sbase_ready, sbase_out = (sem(n) for n in (
            "xs_T", "xsT_ready", "sg_full", "sht_ready", "shg_ready", "su_full", "shh_ready", "sd_full", "sbase_ready", "sbase_out"))

        ids = sb("ids", [P, ND, 2], u32)
        bse, y1s, y2s, s1, fin = (sb(n, [P, ND, D]) for n in ("bse", "y1s", "y2s", "s1", "fin"))
        ids_ready, base_in, y1_in, y2_in, s1_ready, fin_ready, stored = (
            [sem(f"{n}{k}") for k in range(ND)] for n in ("ids_ready", "base_in", "y1_in", "y2_in", "s1_ready", "fin_ready", "stored"))

        PAIRS = NT // 2
        x3_v, x4_v, base_v = (d.rearrange("(g p) d -> p g d", p=P) for d in (x3_d, x4_d, base_d))

        def pair_turns(eng, first, turn, last):
            first()
            with eng.Fori(0, PAIRS // 2 - 1) as t:
                turn(t * 2 + 1, 1, t)
                turn(t * 2 + 2, 0, t + 1)
            last()

        PIECES = [(j, 0, P, 2) for j in range(len(SC) // 2 - 1)] + [(len(SC) // 2 - 1, 0, P, 1), (len(SC) // 2 - 1, 1, SC[-1][1], 1)]

        def piece(buf, j, at, rows, n):
            return buf[0:rows, 2 * j + at:2 * j + at + n, :, :].rearrange("p n k t -> p (n k t)")

        def in_bank(bank, at, rows, n):
            return bank[0:rows, at * 2 * P:(at + n) * 2 * P]

        with nc.Block() as block:

            @block.sync
            def _(sp_):
                for k in range(ND):
                    sp_.sem_inc(row_free[k], 1)
                for s in (xs_T, xsT_ready, shg_ready, shh_ready):
                    sp_.sem_inc(s, 1)
                sp_.sem_inc(sbase_ready, 2)
                sp_.sem_inc(sbase_out, 16)
                with sp_.Fori(0, NT // ND) as t:
                    for q in range(2):
                        for k in (2 * q, 2 * q + 1):
                            sp_.wait_ge(row_free[k], t + 1)
                            sp_.dma_start(xrow[:, k, :], x4_d[bass.ds((t * ND + k) * P, P), :]).then_inc(row_in[k], 16)
                        p = t * 2 + q
                        sp_.wait_ge(xs_T, p + 1)
                        sp_.dma_start(xs[:, :, :], x4_v[:, bass.ds(p * 2, 2), :]).then_inc(xs_in[q], 16)
                        sp_.wait_ge(sbase_ready, p + 1)
                        sp_.dma_start(x3s[:, q, :, :], x3_v[:, bass.ds(p * 2, 2), :]).then_inc(x3s_in[q], 16)
                sp_.wait_ge(w_loaded, 16 * E * (1 + len(IC)))

            @block.gpsimd
            def _(pool):
                g = nc.gpsimd
                g.memset(tri[:, :], 1.0).then_inc(ones_made, 1)
                g.memset(ones[:, :], 1.0).then_inc(ones_made, 1)
                g.memset(ones_p[:, :], 1.0).then_inc(ones_made, 1)
                pool.wait_ge(ones_made, 3)
                g.affine_select(out=tri[:, :], in_=tri[:, :], compare_op=ALU.is_gt, fill=0.0, base=0,
                                pattern=[[1, P]], channel_multiplier=-1).then_inc(tri_made, 1)
                g.iota(tstart[:, :], pattern=[[P, SLOTS_T]], base=0, channel_multiplier=0,
                       allow_small_or_imprecise_dtypes=True).then_inc(tst_made, 1)
                pool.wait_ge(pos_ready, 1)
                with pool.Fori(0, NT // ND) as t:
                    for k in range(ND):
                        pool.wait_ge(row_in[k], t * 16 + 16)
                        for w in range(2):
                            last = g.tensor_copy(idx[:, k, w:w + 1], pos[:, w, bass.ds(t * ND + k, 1)])
                        last.then_inc(idx_copied[k], 1)
                        pool.wait_ge(idx_copied[k], t + 1)
                        pool.sem_inc(waited, 1)
                        for w in range(2):
                            g.indirect_dma_start(xs_d, bass.IndirectOffsetOnAxis(idx[:, k, w:w + 1], 0), xrow[:, k, :], None)\
                                .then_inc(dispatched[k], 16)
                    for k in range(ND):
                        pool.wait_ge(dispatched[k], t * 32 + 32)
                        pool.sem_inc(row_free[k], 1)

            @block.tensor
            def _(pe):
                pe.wait_ge(both_made, 1)
                pe.wait_ge(tri_made, 1)
                bf = both[:, :, :].rearrange("p t e -> p (t e)")
                nc.tensor.matmul(banks[0][:, :], tri[:, :], bf, start=True, stop=True).then_inc(counted, 1)
                nc.tensor.matmul(banks[1][:, :], ones_p[:, :], bf, start=True, stop=True).then_inc(counted, 1)
                mm, tr = nc.tensor.matmul, nc.tensor.transpose
                pe.wait_ge(pos_ready, 1)

                def rows_in(p, par, i):
                    pe.wait_ge(xs_in[par], i * 16 + 16)
                    pe.wait_ge(xsT_ready, p + 1)
                    for k in range(2):
                        for c in range(DC):
                            last = tr(banks[6][:, (k * DC + c) * P:(k * DC + c + 1) * P], xs[:, k, c * P:(c + 1) * P], ident[:, :])
                    last.then_inc(xs_T, 1)

                def gate_up(p, par):
                    pe.wait_ge(xsT_ready, p + 2)
                    for half, full, read in ((0, sg_full, shg_ready), (1, su_full, shh_ready)):
                        pe.wait_ge(read, p + 1)
                        for n, (at, size) in enumerate(SC):
                            for c in range(DC):
                                last = mm(banks[half * 3 + n // 2][0:size, (n % 2) * 2 * P:(n % 2 + 1) * 2 * P],
                                          w_su[:, c, half * SI + at:half * SI + at + size],
                                          xsT[:, par, :, c, :], start=c == 0, stop=c == DC - 1)
                            if n % 2:
                                last.then_inc(full, 1)

                def down(p, par):
                    pe.wait_ge(shh_ready, p + 2)
                    pe.wait_ge(sbase_ready, p + 2)
                    for k in range(2):
                        for n, (at, size) in enumerate(SC):
                            last = mm(banks[7][:, k * D:(k + 1) * D], shh[0:size, par, n, k, :], w_sd[0:size, n, :],
                                      start=n == 0, stop=n == len(SC) - 1)
                    last.then_inc(sd_full, 1)

                def first():
                    rows_in(0, 0, 0)
                    gate_up(0, 0)
                    rows_in(1, 1, 0)

                def turn(p, par, i):
                    gate_up(p, par)
                    rows_in(p + 1, 1 - par, i + par)
                    down(p - 1, 1 - par)

                def last_():
                    gate_up(PAIRS - 1, 1)
                    down(PAIRS - 2, 0)
                    down(PAIRS - 1, 1)

                pair_turns(pe, first, turn, last_)

            @block.scalar
            def _(act):
                f = nc.scalar.activation

                def gate(p):
                    for j, at, rows, n in PIECES:
                        act.wait_ge(sg_full, p * 3 + j + 1)
                        last = f(piece(sht, j, at, rows, n), in_bank(banks[j], at, rows, n), ACT.Tanh, scale=0.5)
                        if at or n == 2:
                            last.then_inc(sht_ready, 1)

                def rows_in(p, par):
                    act.wait_ge(xs_T, p + 2)
                    f(xsT[:, par, :, :, :], banks[6][:, :].rearrange("p (k c t) -> p k c t", k=2, c=DC), ACT.Copy).then_inc(xsT_ready, 1)

                def store(p):
                    act.wait_ge(sbase_ready, p + 3)
                    act.dma_start(base_v[:, bass.ds(p * 2, 2), :], sbase[:, :, :]).then_inc(sbase_out, 16)

                def first():
                    rows_in(0, 0)
                    gate(0)
                    rows_in(1, 1)
                    load_weights()

                def turn(p, par, i):
                    gate(p)
                    rows_in(p + 1, 1 - par)
                    store(p - 1)

                def load_weights():
                    gu_v = a["e_gu"].rearrange("e (c p) n -> e p c n", p=P)
                    for e in range(E):
                        act.dma_start(w_gu[:, e, :, :], gu_v[e, :, :, :]).then_inc(w_loaded, 16)
                        for k, (at, size) in enumerate(IC):
                            act.dma_start(w_dn[0:size, e, k, :], a["e_dn"][e, at:at + size, :]).then_inc(w_loaded, 16)

                def last_():
                    gate(PAIRS - 1)
                    store(PAIRS - 2)
                    store(PAIRS - 1)

                pair_turns(act, first, turn, last_)
                act.wait_ge(sbase_out, 16 * (PAIRS + 1))

            @block.vector
            def _(dve):
                v = nc.vector
                n = [0]

                def link(ins):
                    n[0] += 1
                    ins.then_inc(chain, 1)
                    dve.wait_ge(chain, n[0])

                v.tensor_tensor(both[:, :, :], oh[:, 0, :, :], oh[:, 1, :, :], ALU.add).then_inc(both_made, 1)
                dve.wait_ge(counted, 2)
                dve.wait_ge(ones_made, 3)
                link(v.tensor_copy(cnt[:, :, :], banks[1][:, :].rearrange("p (t e) -> p t e", e=E)))
                for e in range(E):
                    last = v.tensor_tensor_scan(run[:, :, e], ones[:, :], cnt[:, :, e], 0.0, ALU.mult, ALU.add)
                link(last)
                link(v.tensor_scalar(padf[:, :], run[:, NT - 1, :], float(P - 1), None, ALU.add))
                link(v.tensor_copy(padi[:, :], padf[:, :]))
                link(v.tensor_scalar(padi[:, :], padi[:, :], -P, None, ALU.bitwise_and))
                link(v.tensor_copy(padded[:, :], padi[:, :]))
                link(v.tensor_tensor_scan(ends[:, :], ones[:, 0:E], padded[:, :], 0.0, ALU.mult, ALU.add))
                link(v.tensor_tensor(offs[:, :], ends[:, :], padded[:, :], ALU.subtract))
                link(v.tensor_tensor(slot[:, :, :], run[:, :, :], cnt[:, :, :], ALU.subtract))
                link(v.tensor_tensor(slot[:, :, :], slot[:, :, :], banks[0][:, :].rearrange("p (t e) -> p t e", e=E), ALU.add))
                link(v.tensor_tensor(slot[:, :, :], slot[:, :, :], offs[:, :].unsqueeze(1).broadcast_to([P, NT, E]), ALU.add))
                for w in range(2):
                    link(v.tensor_tensor(prod[:, :, :], slot[:, :, :], oh[:, w, :, :], ALU.mult))
                    link(v.tensor_reduce(posf[:, w, :], prod[:, :, :], AX.X, ALU.add))
                v.tensor_copy(pos[:, :, :], posf[:, :, :]).then_inc(pos_ready, 1)
                dve.wait_ge(tst_made, 1)
                link(v.tensor_scalar(eid[:, :], tstart[:, :], ends[0:1, 0:1], None, ALU.is_ge))
                for e in range(1, E - 1):
                    link(v.scalar_tensor_tensor(eid[:, :], tstart[:, :], ends[0:1, e:e + 1], eid[:, :], ALU.is_ge, ALU.add))
                link(v.tensor_copy(eidi[:, :], eid[:, :]))

                def hidden(p, par):
                    dve.wait_ge(shh_ready, p + 1)
                    for j, at, rows, n in PIECES:
                        dve.wait_ge(sht_ready, p * 3 + j + 1)
                        last = v.scalar_tensor_tensor(piece(shg, j, at, rows, n), piece(sht, j, at, rows, n), 1.0,
                                                      in_bank(banks[j], at, rows, n), ALU.add, ALU.mult)
                    last.then_inc(shg_ready, 1)
                    dve.wait_ge(shg_ready, p + 2)
                    for j, at, rows, n in PIECES:
                        dve.wait_ge(su_full, p * 3 + j + 1)
                        last = v.scalar_tensor_tensor(piece(shh[:, par], j, at, rows, n), piece(shg, j, at, rows, n), 0.5,
                                                      in_bank(banks[3 + j], at, rows, n), ALU.mult, ALU.mult)
                    last.then_inc(shh_ready, 1)

                def base(p, par, i):
                    dve.wait_ge(sd_full, p + 1)
                    dve.wait_ge(x3s_in[par], i * 16 + 16)
                    dve.wait_ge(sbase_out, p * 16 + 16)
                    for k in range(2):
                        last = v.scalar_tensor_tensor(sbase[:, k, :], banks[7][:, k * D:(k + 1) * D], sharew[:, bass.ds(p * 2 + k, 1)],
                                                      x3s[:, par, k, :], ALU.mult, ALU.add)
                    last.then_inc(sbase_ready, 1)

                def first():
                    hidden(0, 0)

                def turn(p, par, i):
                    hidden(p, par)
                    base(p - 1, 1 - par, i if par else i - 1)

                def last_():
                    hidden(PAIRS - 1, 1)
                    base(PAIRS - 2, 0, PAIRS // 2 - 1)
                    base(PAIRS - 1, 1, PAIRS // 2 - 1)

                pair_turns(dve, first, turn, last_)

        freeing = (xeT_ready, gg_ready, hh_ready, hT_ready, ye_ready, xe_T, h_T, y_full, gt_ready)
        with nc.Block() as block:
            @block.sync
            def _(sp_):
                for k in range(2):
                    for s in freeing:
                        sp_.sem_inc(s[k], 2 if s is ye_ready else 1)
                    sp_.sem_inc(ye_out[k], 16)
                with sp_.Fori(0, SLOTS_T // 2) as t:
                    for k in range(2):
                        sp_.wait_ge(xe_T[k], t + 1)
                        sp_.dma_start(xe[:, k, :], xs_d[bass.ds((t * 2 + k) * P, P), :]).then_inc(xe_in[k], 16)

            def expert_turns(eng, gate_up, rows_in, down, hidden):
                def turn(*tiles):
                    for step, tile in zip((gate_up, rows_in, down, hidden), tiles):
                        if tile:
                            step(*tile)

                rows_in(0, 0)
                turn((0, 0), (1, 0))
                turn((1, 0), (0, 1), None, (0, 0))
                with eng.Fori(0, SLOTS_T // 2 - 2) as t:
                    turn((0, t + 1), (1, t + 1), (0, t), (1, t))
                    turn((1, t + 1), (0, t + 2), (1, t), (0, t + 1))
                turn((0, LAST), (1, LAST), (0, LAST - 1), (1, LAST - 1))
                turn((1, LAST), None, (1, LAST - 1), (0, LAST))
                turn(None, None, (0, LAST), (1, LAST))
                down(1, LAST)

            LAST = SLOTS_T // 2 - 1

            @block.tensor
            def _(pe):
                mm, tr = nc.tensor.matmul, nc.tensor.transpose

                def expert_of(k, i):
                    return pe.value_load(eidi[0:1, bass.ds(i * 2 + k, 1)], min_val=0, max_val=E - 1)

                def rows_in(k, i):
                    pe.wait_ge(xe_in[k], i * 16 + 16)
                    pe.wait_ge(ye_ready[k], i + 1)
                    for c in range(DC):
                        last = tr(banks[4 + k][:, c * P:(c + 1) * P], xe[:, k, c * P:(c + 1) * P], ident[:, :])
                    last.then_inc(xe_T[k], 1)

                def gate_up(k, i):
                    e = expert_of(k, i)
                    pe.wait_ge(xeT_ready[k], i + 2)
                    pe.wait_ge(hh_ready[k], i + 1)
                    for half, full in ((0, g_full), (1, u_full)):
                        for c in range(DC):
                            last = mm(banks[2 * k + half][:, 0:I], xeT[:, k, c, :],
                                      w_gu[:, bass.ds(e, 1), c, half * I:(half + 1) * I].rearrange("p a n -> p (a n)"),
                                      start=c == 0, stop=c == DC - 1)
                        last.then_inc(full[k], 1)

                def hidden(k, i):
                    pe.wait_ge(hh_ready[k], i + 2)
                    pe.wait_ge(hT_ready[k], i + 1)
                    for n, (at, size) in enumerate(IC):
                        last = tr(banks[6 + k][0:size, n * P:(n + 1) * P], hh[:, k, at:at + size], ident[:, :])
                    last.then_inc(h_T[k], 1)

                def down(k, i):
                    e = expert_of(k, i)
                    pe.wait_ge(hT_ready[k], i + 2)
                    for n, (at, size) in enumerate(IC):
                        last = mm(banks[4 + k][:, 0:D], hT[0:size, k, n, :],
                                  w_dn[0:size, bass.ds(e, 1), n, :].rearrange("p a n -> p (a n)"),
                                  start=n == 0, stop=n == len(IC) - 1)
                    last.then_inc(y_full[k], 1)

                expert_turns(pe, gate_up, rows_in, down, hidden)

            @block.scalar
            def _(act):
                f = nc.scalar.activation

                def rows_in(k, i):
                    act.wait_ge(xe_T[k], i + 2)
                    f(xeT[:, k, :, :], banks[4 + k][:, 0:D].rearrange("p (c n) -> p c n", c=DC), ACT.Copy).then_inc(xeT_ready[k], 1)

                def gate(k, i):
                    act.wait_ge(g_full[k], i + 1)
                    f(gt[:, k, :], banks[2 * k][:, 0:I], ACT.Tanh, scale=0.5).then_inc(gt_ready[k], 1)

                def hidden(k, i):
                    act.wait_ge(h_T[k], i + 2)
                    f(hT[:, k, 0:2, :], banks[6 + k][:, 0:2 * P].rearrange("p (c n) -> p c n", c=2), ACT.Copy)
                    f(hT[0:IC[2][1], k, 2, :], banks[6 + k][0:IC[2][1], 2 * P:3 * P], ACT.Copy).then_inc(hT_ready[k], 1)

                def result(k, i):
                    act.wait_ge(y_full[k], i + 2)
                    act.wait_ge(ye_out[k], i * 16 + 16)
                    f(ye[:, k, :], banks[4 + k][:, 0:D], ACT.Copy).then_inc(ye_ready[k], 1)
                    act.wait_ge(ye_ready[k], i + 3)
                    act.dma_start(ys_d[bass.ds((i * 2 + k) * P, P), :], ye[:, k, :]).then_inc(ye_out[k], 16)

                expert_turns(act, gate, rows_in, result, hidden)
                for k in range(2):
                    act.wait_ge(ye_out[k], 16 + 16 * (SLOTS_T // 2))

            @block.vector
            def _(dve):
                v = nc.vector
                with dve.Fori(0, SLOTS_T // 2) as t:
                    for k in range(2):
                        dve.wait_ge(gt_ready[k], t + 2)
                        v.scalar_tensor_tensor(gg[:, k, :], gt[:, k, :], 1.0, banks[2 * k][:, 0:I], ALU.add, ALU.mult)\
                            .then_inc(gg_ready[k], 1)
                        dve.wait_ge(gg_ready[k], t + 2)
                        dve.wait_ge(u_full[k], t + 1)
                        v.scalar_tensor_tensor(hh[:, k, :], gg[:, k, :], 0.5, banks[2 * k + 1][:, 0:I], ALU.mult, ALU.mult)\
                            .then_inc(hh_ready[k], 1)

        flat = out.rearrange("b t d -> (b t) d")
        with nc.Block() as block:
            @block.sync
            def _(sp_):
                for k in range(ND):
                    for s in (s1_ready, fin_ready, ids_ready):
                        sp_.sem_inc(s[k], 1)
                    sp_.sem_inc(stored[k], 16)
                with sp_.Fori(0, NT // ND) as t:
                    for k in range(ND):
                        sp_.wait_ge(s1_ready[k], t + 1)
                        sp_.dma_start(bse[:, k, :], base_d[bass.ds((t * ND + k) * P, P), :]).then_inc(base_in[k], 16)

            @block.gpsimd
            def _(pool):
                g = nc.gpsimd
                with pool.Fori(0, NT // ND) as t:
                    for k in range(ND):
                        pool.wait_ge(fin_ready[k], t + 1)
                        for w in range(2):
                            last = g.tensor_copy(ids[:, k, w:w + 1], pos[:, w, bass.ds(t * ND + k, 1)])
                        last.then_inc(ids_ready[k], 1)
                        pool.wait_ge(ids_ready[k], t + 2)
                        pool.sem_inc(waited, 1)
                        for w, (ys, s) in enumerate(((y1s, y1_in), (y2s, y2_in))):
                            g.indirect_dma_start(ys[:, k, :], None, ys_d, bass.IndirectOffsetOnAxis(ids[:, k, w:w + 1], 0))\
                                .then_inc(s[k], 16)

            @block.vector
            def _(dve):
                v = nc.vector
                with dve.Fori(0, NT // ND) as t:
                    for k in range(ND):
                        dve.wait_ge(base_in[k], t * 16 + 16)
                        dve.wait_ge(y1_in[k], t * 16 + 16)
                        v.scalar_tensor_tensor(s1[:, k, :], y1s[:, k, :], wcol(topw, t * ND + k, 0), bse[:, k, :], ALU.mult, ALU.add)\
                            .then_inc(s1_ready[k], 1)
                        dve.wait_ge(s1_ready[k], t + 2)
                        dve.wait_ge(y2_in[k], t * 16 + 16)
                        dve.wait_ge(stored[k], t * 16 + 16)
                        v.scalar_tensor_tensor(fin[:, k, :], y2s[:, k, :], wcol(topw, t * ND + k, 1), s1[:, k, :], ALU.mult, ALU.add)\
                            .then_inc(fin_ready[k], 1)

            @block.scalar
            def _(act):
                with act.Fori(0, NT // ND) as t:
                    for k in range(ND):
                        act.wait_ge(fin_ready[k], t + 2)
                        act.dma_start(flat[bass.ds((t * ND + k) * P, P), :], fin[:, k, :]).then_inc(stored[k], 16)
                for k in range(ND):
                    act.wait_ge(stored[k], 16 + 16 * (NT // ND))


def wcol(topw, i, w):
    return topw[:, bass.ds(i, 1), w:w + 1].rearrange("p a b -> p (a b)")


def kernel(L0_attn_x, L0_attn_w_lhs, L0_attn_w_rhs, L0_ffn_kernel, L0_ffn_input_scale, L0_ffn_kernel_scale, L0_ffn_bias,
           L1_attn_norm_w, L1_attn_norm_b, L1_attn_in_proj_w, L1_attn_in_proj_b, L1_attn_conv_w, L1_attn_conv_b,
           L1_attn_x_proj_w, L1_attn_x_proj_b, L1_attn_dt_proj_w, L1_attn_dt_proj_b, L1_attn_A_log, L1_attn_D_param,
           L1_attn_out_proj_w, L1_attn_out_proj_b, L1_ffn_gate_w, L1_ffn_experts_gate_up, L1_ffn_experts_down,
           L1_ffn_shared_gate_w, L1_ffn_shared_up_w, L1_ffn_shared_down_w, L1_ffn_shared_expert_gate_w):
    import numpy as np
    import concourse.bacc as bacc
    from concourse.bass_utils import run_bass_kernel_spmd

    def t(w):
        return np.swapaxes(np.asarray(w), -1, -2)

    def column(vec):
        return np.asarray(vec).reshape(-1, P).T

    given = dict(
        x=L0_attn_x, w_lhs=column(L0_attn_w_lhs), w_rhs=column(L0_attn_w_rhs), kernel=L0_ffn_kernel, s_in=L0_ffn_input_scale,
        s_k=L0_ffn_kernel_scale, fbias=L0_ffn_bias, norm_w=column(L1_attn_norm_w), norm_b=column(L1_attn_norm_b),
        w_in=t(L1_attn_in_proj_w), in_b=column(L1_attn_in_proj_b), conv_w=L1_attn_conv_w, conv_b=column(L1_attn_conv_b),
        w_x=t(L1_attn_x_proj_w), x_bb=np.asarray(L1_attn_x_proj_b)[:NS].reshape(NS, 1), x_bc=np.asarray(L1_attn_x_proj_b)[NS:],
        w_dt=t(L1_attn_dt_proj_w), dt_b=column(L1_attn_dt_proj_b), a_log=L1_attn_A_log, d_param=column(L1_attn_D_param),
        w_out=t(L1_attn_out_proj_w), out_b=L1_attn_out_proj_b,
        w_gate=np.concatenate([t(L1_ffn_gate_w), t(L1_ffn_shared_expert_gate_w)], 1),
        e_gu=t(L1_ffn_experts_gate_up), e_dn=t(L1_ffn_experts_down),
        s_g=t(L1_ffn_shared_gate_w), s_u=t(L1_ffn_shared_up_w), s_dn=t(L1_ffn_shared_down_w))
    nc = bacc.Bacc("TRN2", target_bir_lowering=False, num_devices=1)
    arrays, aps = {}, {}
    for name, value in given.items():
        value = np.ascontiguousarray(value)
        arrays[f"in_{name}"] = value
        aps[name] = nc.dram_tensor(f"in_{name}", value.shape, mybir.dt.from_np(value.dtype), kind="ExternalInput").ap()
    out = nc.dram_tensor("out", (NB, T, D), fp32, kind="ExternalOutput").ap()
    build(nc, aps, out)
    r = run_bass_kernel_spmd(nc, [arrays], core_ids=[0])
    return r.results[0]["out"]
```
